# Optimizing a Trainium2 kernel written in Bass

```python
import numpy as np
import jax
import jax.numpy as jnp

def _softmax(x, axis=-1):
    return jax.nn.softmax(x, axis=axis)

def _gelu(x):
    return jax.nn.gelu(x, approximate=True)

def _silu(x):
    return jax.nn.silu(x)

def _sigmoid(x):
    return jax.nn.sigmoid(x)

def _layernorm(x, axis=-1, eps=1e-05):
    m = jnp.mean(x, axis=axis, keepdims=True)
    v = jnp.var(x, axis=axis, keepdims=True)
    return (x - m) / jnp.sqrt(v + eps)

def _scatter_add(tgt, idx, src, axis=0):
    return tgt.at[idx].add(src)

def _segment_sum(src, seg, n):
    return jax.ops.segment_sum(src, seg, n)
kernel_name = 'mk_conv_preact_d4_conv_nhwc768_r4_536b5c'

def setup_inputs(seed: int=0):
    np.random.seed(seed)
    _w = jnp.asarray

    def _rec_inputs():
        import jax
        import jax.numpy as jnp
        _gk = jax.random.key(seed)
        x = -0.0005963 + 1.001 * jax.random.normal(jax.random.fold_in(_gk, 1), (1, 16, 16, 192), jnp.float32)
        return x
    x = _rec_inputs()

    def _L0_conv_setup():
        import jax, jax.numpy as jnp
        import numpy as np
        NUM_HEADS = 12

        def _rel_table(size, rel_pos):
            coords = jnp.arange(size)[:, None] - jnp.arange(size)[None, :] + (size - 1)
            return rel_pos[coords]
        key = jax.random.key(seed)
        ks = jax.random.split(key, 7)
        B, H, W, C = (1, 16, 16, 192)
        hd = C // NUM_HEADS
        return {'x': jax.random.normal(ks[0], (B, H, W, C), dtype=jnp.float32), 'qkv_w': jax.random.normal(ks[1], (C, 3 * C), dtype=jnp.float32) * 0.02, 'qkv_b': jax.random.normal(ks[2], (3 * C,), dtype=jnp.float32) * 0.02, 'proj_w': jax.random.normal(ks[3], (C, C), dtype=jnp.float32) * 0.02, 'proj_b': jax.random.normal(ks[4], (C,), dtype=jnp.float32) * 0.02, 'rel_pos_h': jax.random.normal(ks[5], (2 * H - 1, hd), dtype=jnp.float32) * 0.02, 'rel_pos_w': jax.random.normal(ks[6], (2 * W - 1, hd), dtype=jnp.float32) * 0.02}
    _L0_conv_all = _L0_conv_setup()
    _L0_conv_in = {k: v for k, v in _L0_conv_all.items() if k in ('qkv_w', 'qkv_b', 'proj_w', 'proj_b', 'rel_pos_h', 'rel_pos_w')}
    del _L0_conv_all

    def _L1_conv_setup():
        import jax, jax.numpy as jnp
        import numpy as np
        D_MODEL = 192
        N_HEADS = 12
        HEAD_DIM = D_MODEL // N_HEADS
        FFN_DIM = 768
        MAX_WAVELENGTH = 10000.0
        ROPE_PERCENT = 0.5
        NORM_EPS = 1e-05

        def _layernorm(x, g, b):
            mu = jnp.mean(x, axis=-1, keepdims=True)
            var = jnp.mean(jnp.square(x - mu), axis=-1, keepdims=True)
            return (x - mu) * jax.lax.rsqrt(var + NORM_EPS) * g + b

        def _apply_p_rope(x, positions):
            half = HEAD_DIM // 2
            rope_angles = int(ROPE_PERCENT * HEAD_DIM) // 2
            fraction = 2.0 * jnp.arange(rope_angles, dtype=jnp.float32) / HEAD_DIM
            timescale = jnp.concatenate([MAX_WAVELENGTH ** fraction, jnp.full((half - rope_angles,), jnp.inf, dtype=jnp.float32)])
            angles = positions[:, None].astype(jnp.float32) / timescale[None, :]
            sin = jnp.sin(angles)[None, None]
            cos = jnp.cos(angles)[None, None]
            x1, x2 = jnp.split(x, 2, axis=-1)
            return jnp.concatenate([x1 * cos - x2 * sin, x2 * cos + x1 * sin], axis=-1)

        def _forward(hidden_state, wq, bq, wk, bk, wv, bv, wo, bo, attn_biases, ln1_g, ln1_b, ln3_g, ln3_b, w1, b1, w2, b2):
            B, C, S, D = hidden_state.shape
            T = C * S
            flat = hidden_state.reshape(B, T, D)
            ni = _layernorm(flat, ln1_g, ln1_b)
            scaling = HEAD_DIM ** (-0.5)
            q = (ni @ wq + bq) * scaling
            k = ni @ wk + bk
            v = ni @ wv + bv
            to_heads = lambda t: t.reshape(B, T, N_HEADS, HEAD_DIM).transpose(0, 2, 1, 3)
            q, k, v = (to_heads(q), to_heads(k), to_heads(v))
            positions = jnp.arange(T)
            k = _apply_p_rope(k, positions)
            q = _apply_p_rope(q, positions)
            scores = jnp.einsum('bhtd,bhsd->bhts', q, k)
            variate_ids = positions // S
            same = (variate_ids[:, None] == variate_ids[None, :]).astype(scores.dtype)
            variate_bias = same[None, :, :] * attn_biases[:, 0][:, None, None] + (1.0 - same[None, :, :]) * attn_biases[:, 1][:, None, None]
            scores = scores + variate_bias[None]
            probs = jax.nn.softmax(scores, axis=-1)
            attn = jnp.einsum('bhts,bhsd->bhtd', probs, v)
            attn = attn.transpose(0, 2, 1, 3).reshape(B, T, D)
            attn = attn @ wo + bo
            flat = flat + attn
            ff_in = _layernorm(flat, ln3_g, ln3_b)
            ff = jax.nn.gelu(ff_in @ w1 + b1, approximate=False) @ w2 + b2
            flat = flat + ff
            return flat.reshape(B, C, S, D)
        key = jax.random.key(seed)
        ks = jax.random.split(key, 12)
        B, C, S = (2, 16, 32)
        init = lambda k, shape: jax.random.normal(k, shape, dtype=jnp.float32) * 0.02
        return {'hidden_state': jax.random.normal(ks[0], (B, C, S, D_MODEL), dtype=jnp.float32), 'wq': init(ks[1], (D_MODEL, D_MODEL)), 'bq': jnp.zeros((D_MODEL,), jnp.float32), 'wk': init(ks[2], (D_MODEL, D_MODEL)), 'bk': jnp.zeros((D_MODEL,), jnp.float32), 'wv': init(ks[3], (D_MODEL, D_MODEL)), 'bv': jnp.zeros((D_MODEL,), jnp.float32), 'wo': init(ks[4], (D_MODEL, D_MODEL)), 'bo': jnp.zeros((D_MODEL,), jnp.float32), 'attn_biases': init(ks[5], (N_HEADS, 2)), 'ln1_g': jnp.ones((D_MODEL,), jnp.float32), 'ln1_b': jnp.zeros((D_MODEL,), jnp.float32), 'ln3_g': jnp.ones((D_MODEL,), jnp.float32), 'ln3_b': jnp.zeros((D_MODEL,), jnp.float32), 'w1': init(ks[6], (D_MODEL, FFN_DIM)), 'b1': jnp.zeros((FFN_DIM,), jnp.float32), 'w2': init(ks[7], (FFN_DIM, D_MODEL)), 'b2': jnp.zeros((D_MODEL,), jnp.float32)}
    _L1_conv_all = _L1_conv_setup()
    _L1_conv_in = {k: v for k, v in _L1_conv_all.items() if k in ('wq', 'bq', 'wk', 'bk', 'wv', 'bv', 'wo', 'bo', 'attn_biases', 'ln1_g', 'ln1_b', 'ln3_g', 'ln3_b', 'w1', 'b1', 'w2', 'b2')}
    del _L1_conv_all

    def _L2_conv_setup():
        import jax, jax.numpy as jnp
        import numpy as np
        D_MODEL = 192
        D_HEAD = 16
        N_HEADS = D_MODEL // D_HEAD
        KERNEL = 7
        NEG_INF = -1e+30

        def make_neighbourhood_mask(kernel_h, kernel_w, canvas_h, canvas_w):
            h_ramp = jnp.arange(canvas_h)
            w_ramp = jnp.arange(canvas_w)
            h_pos, w_pos = jnp.meshgrid(h_ramp, w_ramp, indexing='ij')
            start_h = jnp.clip(h_pos - kernel_h // 2, 0, canvas_h - kernel_h)[..., None, None]
            end_h = start_h + kernel_h
            start_w = jnp.clip(w_pos - kernel_w // 2, 0, canvas_w - kernel_w)[..., None, None]
            end_w = start_w + kernel_w
            h_range = h_ramp.reshape(1, 1, canvas_h, 1)
            w_range = w_ramp.reshape(1, 1, 1, canvas_w)
            mask = (h_range >= start_h) & (h_range < end_h) & (w_range >= start_w) & (w_range < end_w)
            return mask.reshape(canvas_h * canvas_w, canvas_h * canvas_w)
        key = jax.random.key(seed)
        k1, k2, k3, k4, k5, k6 = jax.random.split(key, 6)
        x = jax.random.normal(k1, (2, 48, 48, D_MODEL), dtype=jnp.float32)
        registers = jax.random.normal(k2, (16, D_MODEL), dtype=jnp.float32)
        scale = 1.0 / np.sqrt(D_MODEL)
        qkv_w = jax.random.normal(k3, (3 * D_MODEL, D_MODEL), dtype=jnp.float32) * scale
        qkv_b = jax.random.normal(k4, (3 * D_MODEL,), dtype=jnp.float32) * 0.01
        out_w = jax.random.normal(k5, (D_MODEL, D_MODEL), dtype=jnp.float32) * scale
        out_b = jax.random.normal(k6, (D_MODEL,), dtype=jnp.float32) * 0.01
        return {'x': x, 'registers': registers, 'qkv_w': qkv_w, 'qkv_b': qkv_b, 'out_w': out_w, 'out_b': out_b}
    _L2_conv_all = _L2_conv_setup()
    _L2_conv_in = {k: v for k, v in _L2_conv_all.items() if k in ('registers', 'qkv_w', 'qkv_b', 'out_w', 'out_b')}
    del _L2_conv_all

    def _L3_conv_setup():
        import jax, jax.numpy as jnp
        import numpy as np
        B, H, W, DIM, NH = (4, 32, 32, 192, 12)
        HD = DIM // NH

        def _get_rel_pos(size, rel_pos):
            idx = jnp.arange(size)[:, None] - jnp.arange(size)[None, :] + (size - 1)
            return rel_pos[idx]
        key = jax.random.key(seed)
        ks = jax.random.split(key, 7)
        s = 0.02
        return {'x': jax.random.normal(ks[0], (B, H, W, DIM), dtype=jnp.float32), 'qkv_w': jax.random.normal(ks[1], (3 * DIM, DIM), dtype=jnp.float32) * s, 'qkv_b': jax.random.normal(ks[2], (3 * DIM,), dtype=jnp.float32) * s, 'proj_w': jax.random.normal(ks[3], (DIM, DIM), dtype=jnp.float32) * s, 'proj_b': jax.random.normal(ks[4], (DIM,), dtype=jnp.float32) * s, 'rel_pos_h': jax.random.normal(ks[5], (2 * H - 1, HD), dtype=jnp.float32) * s, 'rel_pos_w': jax.random.normal(ks[6], (2 * W - 1, HD), dtype=jnp.float32) * s}
    _L3_conv_all = _L3_conv_setup()
    _L3_conv_in = {k: v for k, v in _L3_conv_all.items() if k in ('qkv_w', 'qkv_b', 'proj_w', 'proj_b', 'rel_pos_h', 'rel_pos_w')}
    del _L3_conv_all
    return {'x': x, 'L0_conv_qkv_w': _L0_conv_in['qkv_w'], 'L0_conv_qkv_b': _L0_conv_in['qkv_b'], 'L0_conv_proj_w': _L0_conv_in['proj_w'], 'L0_conv_proj_b': _L0_conv_in['proj_b'], 'L0_conv_rel_pos_h': _L0_conv_in['rel_pos_h'], 'L0_conv_rel_pos_w': _L0_conv_in['rel_pos_w'], 'L1_conv_wq': _L1_conv_in['wq'], 'L1_conv_bq': _L1_conv_in['bq'], 'L1_conv_wk': _L1_conv_in['wk'], 'L1_conv_bk': _L1_conv_in['bk'], 'L1_conv_wv': _L1_conv_in['wv'], 'L1_conv_bv': _L1_conv_in['bv'], 'L1_conv_wo': _L1_conv_in['wo'], 'L1_conv_bo': _L1_conv_in['bo'], 'L1_conv_attn_biases': _L1_conv_in['attn_biases'], 'L1_conv_ln1_g': _L1_conv_in['ln1_g'], 'L1_conv_ln1_b': _L1_conv_in['ln1_b'], 'L1_conv_ln3_g': _L1_conv_in['ln3_g'], 'L1_conv_ln3_b': _L1_conv_in['ln3_b'], 'L1_conv_w1': _L1_conv_in['w1'], 'L1_conv_b1': _L1_conv_in['b1'], 'L1_conv_w2': _L1_conv_in['w2'], 'L1_conv_b2': _L1_conv_in['b2'], 'L2_conv_registers': _L2_conv_in['registers'], 'L2_conv_qkv_w': _L2_conv_in['qkv_w'], 'L2_conv_qkv_b': _L2_conv_in['qkv_b'], 'L2_conv_out_w': _L2_conv_in['out_w'], 'L2_conv_out_b': _L2_conv_in['out_b'], 'L3_conv_qkv_w': _L3_conv_in['qkv_w'], 'L3_conv_qkv_b': _L3_conv_in['qkv_b'], 'L3_conv_proj_w': _L3_conv_in['proj_w'], 'L3_conv_proj_b': _L3_conv_in['proj_b'], 'L3_conv_rel_pos_h': _L3_conv_in['rel_pos_h'], 'L3_conv_rel_pos_w': _L3_conv_in['rel_pos_w']}

def reference(x, L0_conv_qkv_w, L0_conv_qkv_b, L0_conv_proj_w, L0_conv_proj_b, L0_conv_rel_pos_h, L0_conv_rel_pos_w, L1_conv_wq, L1_conv_bq, L1_conv_wk, L1_conv_bk, L1_conv_wv, L1_conv_bv, L1_conv_wo, L1_conv_bo, L1_conv_attn_biases, L1_conv_ln1_g, L1_conv_ln1_b, L1_conv_ln3_g, L1_conv_ln3_b, L1_conv_w1, L1_conv_b1, L1_conv_w2, L1_conv_b2, L2_conv_registers, L2_conv_qkv_w, L2_conv_qkv_b, L2_conv_out_w, L2_conv_out_b, L3_conv_qkv_w, L3_conv_qkv_b, L3_conv_proj_w, L3_conv_proj_b, L3_conv_rel_pos_h, L3_conv_rel_pos_w):
    import jax
    import jax.numpy as jnp

    def _L0_conv_ref(x, qkv_w, qkv_b, proj_w, proj_b, rel_pos_h, rel_pos_w):
        import jax, jax.numpy as jnp
        import numpy as np
        NUM_HEADS = 12

        def _rel_table(size, rel_pos):
            coords = jnp.arange(size)[:, None] - jnp.arange(size)[None, :] + (size - 1)
            return rel_pos[coords]
        B, H, W, C = x.shape
        nh = NUM_HEADS
        hd = C // nh
        scale = hd ** (-0.5)
        N = H * W
        qkv = x.reshape(B, N, C) @ qkv_w + qkv_b
        qkv = qkv.reshape(B, N, 3, nh, hd).transpose(2, 0, 3, 1, 4).reshape(3, B * nh, N, hd)
        q, k, v = (qkv[0], qkv[1], qkv[2])
        attn = jnp.einsum('bqd,bkd->bqk', q * scale, k)
        Rh = _rel_table(H, rel_pos_h)
        Rw = _rel_table(W, rel_pos_w)
        qr = q.reshape(B * nh, H, W, hd)
        rel_h = jnp.einsum('bhwc,hkc->bhwk', qr, Rh)
        rel_w = jnp.einsum('bhwc,wkc->bhwk', qr, Rw)
        bias = rel_h[..., :, None] + rel_w[..., None, :]
        attn = attn + bias.reshape(B * nh, N, N)
        attn = jax.nn.softmax(attn, axis=-1)
        out = jnp.einsum('bqk,bkd->bqd', attn, v)
        out = out.reshape(B, nh, H, W, hd).transpose(0, 2, 3, 1, 4).reshape(B, H, W, C)
        return out @ proj_w + proj_b

    def _L1_conv_ref(hidden_state, wq, bq, wk, bk, wv, bv, wo, bo, attn_biases, ln1_g, ln1_b, ln3_g, ln3_b, w1, b1, w2, b2):
        import jax, jax.numpy as jnp
        import numpy as np
        D_MODEL = 192
        N_HEADS = 12
        HEAD_DIM = D_MODEL // N_HEADS
        FFN_DIM = 768
        MAX_WAVELENGTH = 10000.0
        ROPE_PERCENT = 0.5
        NORM_EPS = 1e-05

        def _layernorm(x, g, b):
            mu = jnp.mean(x, axis=-1, keepdims=True)
            var = jnp.mean(jnp.square(x - mu), axis=-1, keepdims=True)
            return (x - mu) * jax.lax.rsqrt(var + NORM_EPS) * g + b

        def _apply_p_rope(x, positions):
            half = HEAD_DIM // 2
            rope_angles = int(ROPE_PERCENT * HEAD_DIM) // 2
            fraction = 2.0 * jnp.arange(rope_angles, dtype=jnp.float32) / HEAD_DIM
            timescale = jnp.concatenate([MAX_WAVELENGTH ** fraction, jnp.full((half - rope_angles,), jnp.inf, dtype=jnp.float32)])
            angles = positions[:, None].astype(jnp.float32) / timescale[None, :]
            sin = jnp.sin(angles)[None, None]
            cos = jnp.cos(angles)[None, None]
            x1, x2 = jnp.split(x, 2, axis=-1)
            return jnp.concatenate([x1 * cos - x2 * sin, x2 * cos + x1 * sin], axis=-1)

        def _forward(hidden_state, wq, bq, wk, bk, wv, bv, wo, bo, attn_biases, ln1_g, ln1_b, ln3_g, ln3_b, w1, b1, w2, b2):
            B, C, S, D = hidden_state.shape
            T = C * S
            flat = hidden_state.reshape(B, T, D)
            ni = _layernorm(flat, ln1_g, ln1_b)
            scaling = HEAD_DIM ** (-0.5)
            q = (ni @ wq + bq) * scaling
            k = ni @ wk + bk
            v = ni @ wv + bv
            to_heads = lambda t: t.reshape(B, T, N_HEADS, HEAD_DIM).transpose(0, 2, 1, 3)
            q, k, v = (to_heads(q), to_heads(k), to_heads(v))
            positions = jnp.arange(T)
            k = _apply_p_rope(k, positions)
            q = _apply_p_rope(q, positions)
            scores = jnp.einsum('bhtd,bhsd->bhts', q, k)
            variate_ids = positions // S
            same = (variate_ids[:, None] == variate_ids[None, :]).astype(scores.dtype)
            variate_bias = same[None, :, :] * attn_biases[:, 0][:, None, None] + (1.0 - same[None, :, :]) * attn_biases[:, 1][:, None, None]
            scores = scores + variate_bias[None]
            probs = jax.nn.softmax(scores, axis=-1)
            attn = jnp.einsum('bhts,bhsd->bhtd', probs, v)
            attn = attn.transpose(0, 2, 1, 3).reshape(B, T, D)
            attn = attn @ wo + bo
            flat = flat + attn
            ff_in = _layernorm(flat, ln3_g, ln3_b)
            ff = jax.nn.gelu(ff_in @ w1 + b1, approximate=False) @ w2 + b2
            flat = flat + ff
            return flat.reshape(B, C, S, D)
        return _forward(hidden_state, wq, bq, wk, bk, wv, bv, wo, bo, attn_biases, ln1_g, ln1_b, ln3_g, ln3_b, w1, b1, w2, b2)

    def _L2_conv_ref(x, registers, qkv_w, qkv_b, out_w, out_b):
        import jax, jax.numpy as jnp
        import numpy as np
        D_MODEL = 192
        D_HEAD = 16
        N_HEADS = D_MODEL // D_HEAD
        KERNEL = 7
        NEG_INF = -1e+30

        def make_neighbourhood_mask(kernel_h, kernel_w, canvas_h, canvas_w):
            h_ramp = jnp.arange(canvas_h)
            w_ramp = jnp.arange(canvas_w)
            h_pos, w_pos = jnp.meshgrid(h_ramp, w_ramp, indexing='ij')
            start_h = jnp.clip(h_pos - kernel_h // 2, 0, canvas_h - kernel_h)[..., None, None]
            end_h = start_h + kernel_h
            start_w = jnp.clip(w_pos - kernel_w // 2, 0, canvas_w - kernel_w)[..., None, None]
            end_w = start_w + kernel_w
            h_range = h_ramp.reshape(1, 1, canvas_h, 1)
            w_range = w_ramp.reshape(1, 1, 1, canvas_w)
            mask = (h_range >= start_h) & (h_range < end_h) & (w_range >= start_w) & (w_range < end_w)
            return mask.reshape(canvas_h * canvas_w, canvas_h * canvas_w)
        n, h, w, _ = x.shape
        nh, e = (N_HEADS, D_HEAD)
        s = h * w
        r = registers.shape[0]
        qkv = x @ qkv_w.T + qkv_b
        qkv = qkv.reshape(n, h, w, 3, nh, e)
        qkv = qkv.transpose(3, 0, 4, 1, 2, 5).reshape(3, n, nh, s, e)
        q, k, v = (qkv[0], qkv[1], qkv[2])
        reg_kv = registers @ qkv_w[D_MODEL:].T + qkv_b[D_MODEL:]
        reg_kv = reg_kv.reshape(r, 2, nh, e).transpose(1, 2, 0, 3)
        reg_k = jnp.broadcast_to(reg_kv[0][None], (n, nh, r, e))
        reg_v = jnp.broadcast_to(reg_kv[1][None], (n, nh, r, e))
        k_cat = jnp.concatenate([k, reg_k], axis=-2)
        v_cat = jnp.concatenate([v, reg_v], axis=-2)
        mask = make_neighbourhood_mask(KERNEL, KERNEL, h, w)
        mask_cat = jnp.concatenate([mask, jnp.ones((s, r), dtype=bool)], axis=-1)
        scale = 1.0 / jnp.sqrt(jnp.asarray(e, dtype=x.dtype))
        scores = jnp.einsum('bnqe,bnke->bnqk', q, k_cat) * scale
        scores = jnp.where(mask_cat[None, None], scores, NEG_INF)
        attn = jax.nn.softmax(scores, axis=-1)
        o = jnp.einsum('bnqk,bnke->bnqe', attn, v_cat)
        o = o.transpose(0, 2, 1, 3).reshape(n, h, w, nh * e)
        return o @ out_w.T + out_b

    def _L3_conv_ref(x, qkv_w, qkv_b, proj_w, proj_b, rel_pos_h, rel_pos_w):
        import jax, jax.numpy as jnp
        import numpy as np
        B, H, W, DIM, NH = (4, 32, 32, 192, 12)
        HD = DIM // NH

        def _get_rel_pos(size, rel_pos):
            idx = jnp.arange(size)[:, None] - jnp.arange(size)[None, :] + (size - 1)
            return rel_pos[idx]
        b, h, w, c = x.shape
        hw = h * w
        hd = c // NH
        scale = hd ** (-0.5)
        qkv = x @ qkv_w.T + qkv_b
        qkv = qkv.reshape(b, hw, 3, NH, hd).transpose(2, 0, 3, 1, 4)
        q, k, v = (qkv[0], qkv[1], qkv[2])
        Rh = _get_rel_pos(h, rel_pos_h)
        Rw = _get_rel_pos(w, rel_pos_w)
        r_q = q.reshape(b, NH, h, w, hd)
        rel_h = jnp.einsum('bnhwc,hkc->bnhwk', r_q, Rh)
        rel_w = jnp.einsum('bnhwc,wkc->bnhwk', r_q, Rw)
        bias = (rel_h[..., :, None] + rel_w[..., None, :]).reshape(b, NH, hw, hw)
        attn = jnp.einsum('bnqd,bnkd->bnqk', q, k) * scale + bias
        attn = jax.nn.softmax(attn, axis=-1)
        out = jnp.einsum('bnqk,bnkd->bnqd', attn, v)
        out = out.reshape(b, NH, h, w, hd).transpose(0, 2, 3, 1, 4).reshape(b, h, w, c)
        return out @ proj_w.T + proj_b

    def _gn(v, G=32, eps=1e-05):
        B_, H_, W_, C_ = v.shape
        g = v.reshape(B_, H_, W_, G, C_ // G)
        m = jnp.mean(g, axis=(1, 2, 4), keepdims=True)
        s = jnp.var(g, axis=(1, 2, 4), keepdims=True)
        return ((g - m) / jnp.sqrt(s + eps)).reshape(v.shape)

    def _ln_c(v, eps=1e-06):
        m = jnp.mean(v, axis=-1, keepdims=True)
        s = jnp.var(v, axis=-1, keepdims=True)
        return (v - m) / jnp.sqrt(s + eps)

    def _ln_t(v, eps=1e-05):
        m = jnp.mean(v, axis=-1, keepdims=True)
        s = jnp.var(v, axis=-1, keepdims=True)
        return (v - m) / jnp.sqrt(s + eps)

    def _to_tokens(v):
        B_, H_, W_, C_ = v.shape
        return v.reshape(B_, H_ * W_, C_)

    def _from_tokens(t, like):
        return t.reshape(like.shape)
    x = x + _L0_conv_ref(_gn(x), L0_conv_qkv_w, L0_conv_qkv_b, L0_conv_proj_w, L0_conv_proj_b, L0_conv_rel_pos_h, L0_conv_rel_pos_w)
    x = x + _L1_conv_ref(_gn(x), L1_conv_wq, L1_conv_bq, L1_conv_wk, L1_conv_bk, L1_conv_wv, L1_conv_bv, L1_conv_wo, L1_conv_bo, L1_conv_attn_biases, L1_conv_ln1_g, L1_conv_ln1_b, L1_conv_ln3_g, L1_conv_ln3_b, L1_conv_w1, L1_conv_b1, L1_conv_w2, L1_conv_b2)
    x = x + _L2_conv_ref(_gn(x), L2_conv_registers, L2_conv_qkv_w, L2_conv_qkv_b, L2_conv_out_w, L2_conv_out_b)
    x = x + _L3_conv_ref(_gn(x), L3_conv_qkv_w, L3_conv_qkv_b, L3_conv_proj_w, L3_conv_proj_b, L3_conv_rel_pos_h, L3_conv_rel_pos_w)
    return x

_drawn_inputs = setup_inputs


def setup_inputs(seed=0):
    import zlib

    import numpy as np

    out = dict(_drawn_inputs(seed))
    spreads = {'L1_conv_bq': (0.0, 0.8),
     'L1_conv_bk': (0.0, 0.8),
     'L1_conv_bv': (0.0, 0.487),
     'L1_conv_bo': (0.0, 0.353),
     'L1_conv_ln1_g': (1.0, 0.6),
     'L1_conv_ln1_b': (0.0, 0.8),
     'L1_conv_ln3_g': (1.0, 0.6),
     'L1_conv_ln3_b': (0.0, 2.0),
     'L1_conv_b1': (0.0, 0.513),
     'L1_conv_b2': (0.0, 0.299)}
    factors = {'L0_conv_qkv_w': 8.0,
     'L0_conv_qkv_b': 8.0,
     'L0_conv_proj_w': 8.0,
     'L0_conv_proj_b': 3.024,
     'L0_conv_rel_pos_h': 8.0,
     'L0_conv_rel_pos_w': 8.0,
     'L1_conv_wq': 8.0,
     'L1_conv_wk': 8.0,
     'L1_conv_wv': 8.0,
     'L1_conv_wo': 3.139,
     'L1_conv_attn_biases': 42.28,
     'L2_conv_qkv_b': 21.88,
     'L2_conv_out_b': 8.0,
     'L3_conv_qkv_w': 8.0,
     'L3_conv_qkv_b': 8.0,
     'L3_conv_proj_w': 8.0,
     'L3_conv_proj_b': 20.099,
     'L3_conv_rel_pos_h': 8.0,
     'L3_conv_rel_pos_w': 8.0}
    for name, (base, spread) in spreads.items():
        noise = np.random.default_rng([zlib.crc32(name.encode()), seed]).standard_normal(out[name].shape)
        drawn = base * np.exp(spread * noise) if base else spread * noise
        out[name] = jnp.asarray(drawn.astype(out[name].dtype))
    for name, factor in factors.items():
        out[name] = (out[name] * factor).astype(out[name].dtype)
    return out
```

```python
from contextlib import ExitStack

import numpy as np

import concourse.bass as bass
from concourse import mybir
from concourse.alu_op_type import AluOpType as ALU

ACT = mybir.ActivationFunctionType
AX = mybir.AxisListType
F32 = mybir.dt.float32
F32R = mybir.dt.float32r
BF16 = mybir.dt.bfloat16

SIDE = 16
T = SIDE * SIDE
C = 192
CC = 96
NC = C // CC
HD = 16
NH = C // HD
HPC = CC // HD
P = 128
NG = 3
GH = 4
NU = NH // 2
NREG = 16
FF = 768
FM = FF // P
KW = T + 32
GN_GROUP = C // 32
GN_EPS = 1e-5
LN_EPS = 1e-5
NREL = 2 * SIDE - 1
QK_SCALE = HD ** -0.5
MASKED = -1e30
LAYERS = 4
REL_LAYERS = (0, 3)
TERMS = ((0, 0), (0, 1), (1, 0), (0, 2), (1, 1), (2, 0))

VEC = {name: 2 * n for n, name in enumerate(
    [f"{v}{l}" for l in range(LAYERS) for v in ("bq", "bk", "bo")]
    + ["bqp", "bkp", "ln1g", "ln1b", "ln3g", "ln3b", "b2"])}

SEL_ROWS = {"qh": ((0, 16), 1.0), "ql": ((32,), 1.0), "kh": ((0, 32), QK_SCALE), "kl": ((16,), QK_SCALE),
            "rh": ((64,), 1.0), "rl": ((80,), 1.0), "ch": ((96,), 1.0), "cl": ((112,), 1.0)}
SEL_KINDS = tuple(SEL_ROWS)


def build(nc, a, out):
    with ExitStack() as ctx:
        def sb(name, shape, dt=F32):
            return ctx.enter_context(nc.sbuf_tensor(name, shape, dt))

        def ps(name, shape):
            return ctx.enter_context(nc.psum_tensor(name, shape, F32))

        X = sb("X", [CC, NC, T])
        XN = sb("XN", [CC, NC, T])
        FL = sb("FL", [CC, NC, T])
        DV = sb("DV", [CC, NC, T])
        SQ = sb("SQ", [CC, NC, T])
        VE = sb("VE", [CC, T])
        Y0 = sb("Y0", [CC, T])
        YN = sb("YN", [CC, T])
        QF = sb("QF", [CC, NC, T])
        KF = sb("KF", [CC, NC, T])
        QH = sb("QH", [CC, NC, T], F32R)
        QL = sb("QL", [CC, NC, T], F32R)
        KH = sb("KH", [CC, NC, T], F32R)
        KL = sb("KL", [CC, NC, T], F32R)
        QB = sb("QB", [CC, 3, NC, T], BF16)
        QR = sb("QR", [CC, NC, T])
        RF = [sb(f"RF{i}", [CC, NC, T]) for i in range(2)]
        RH = [sb(f"RH{i}", [CC, NC, T], F32R) for i in range(2)]
        RL = [sb(f"RL{i}", [CC, NC, T], F32R) for i in range(2)]
        QS = [sb(f"QS{i}", [P, NH, T], F32R) for i in range(2)]
        KS = sb("KS", [P, NH, KW], F32R)
        VX = sb("VX", [P, 2, NH, 32])
        VR = sb("VR", [P, NH, 32])
        PR = [sb(f"PR{i}", [P, 2, 2 * T]) for i in range(3)]
        PG = [sb(f"PG{i}", [P, T]) for i in range(2)]
        NM = [sb(f"NM{i}", [P, 2, P], F32R) for i in range(2)]
        MT = [sb(f"MT{i}", [P, T], F32R) for i in range(2)]
        U = [sb(f"U{i}", [P, T]) for i in range(2)]
        LD = [sb(f"LD{i}", [P, T]) for i in range(2)]
        RD = [sb(f"RD{i}", [P, T]) for i in range(2)]
        O = [sb(f"O{i}", [P, T]) for i in range(NG)]
        STAT = sb("STAT", [CC, NC, 6])
        MS = sb("MS", [CC, NC, 2])
        GM = sb("GM", [CC, NC, 2])
        GT = sb("GT", [CC, 6, NC])

        WQKV = [sb(f"WQKV{l}", [CC, NC, 3 * C]) for l in range(LAYERS)]
        WP = sb("WP", [CC, NC, 2 * C])
        WO = [sb(f"WO{l}", [P, NG, C]) for l in range(LAYERS)]
        VB = sb("VB", [P, LAYERS, C])
        W1 = sb("W1", [CC, NC, FF])
        W2 = sb("W2", [P, FM, C])
        B1 = sb("B1", [P, FM])
        VECS = sb("VECS", [CC, 2 * len(VEC)])
        RELT = sb("RELT", [CC, 4, HPC * 32])
        RELB = sb("RELB", [CC, 3, 4, HPC * 32], BF16)
        ROPE = sb("ROPE", [CC, 2, T])
        GAVG = sb("GAVG", [CC, CC])
        ONESC = sb("ONESC", [CC, CC])
        HOT = sb("HOT", [P, T])
        MASK = sb("MASK", [P, T])
        BSEL = sb("BSEL", [P, P])
        PCOL = sb("PCOL", [P, 3])
        ABT = sb("ABT", [P, 2, NH])
        ABH = sb("ABH", [P, 2, NH], F32R)
        ABL = sb("ABL", [P, 2, NH])
        ABS = sb("ABS", [P, 3, NH])
        REGT = sb("REGT", [CC, NC, P])
        KRF = sb("KRF", [CC, NC, NREG])
        KRH = sb("KRH", [CC, NC, NREG], F32R)
        KRL = sb("KRL", [CC, NC, NREG], F32R)
        VRB = sb("VRB", [P, C])
        IDF = sb("IDF", [P, P])
        IDR = sb("IDR", [P, P], F32R)
        SEL = sb("SEL", [CC, len(SEL_KINDS), HPC, P], F32R)
        SELM = sb("SELM", [P, GH, P], F32R)
        SELR = sb("SELR", [P, GH, 32])

        RING = [ps(f"RING{i}", [P, 2, 512]) for i in range(2)]
        PA = ps("PA", [P, 512])
        PB = ps("PB", [P, 512])
        PC = [ps(f"PC{i}", [P, 512]) for i in range(2)]

        def hidden(m):
            return PR[m // 4][:, m % 4 // 2, m % 2 * T:(m % 2 + 1) * T]

        PER = [GH if l == 2 else 2 for l in range(LAYERS)]

        def ring_order(l):
            def scores(g):
                return ([("r", l, g)] if l == 2 else []) + [("e", l, 2 * g), ("e", l, 2 * g + 1)]

            found = [("v", l, 0)]
            for g in range(NG):
                found += [("s", l, 2 * g), ("s", l, 2 * g + 1)]
                found += [("m", l, PER[l] * g + i) for i in range(PER[l])]
                if g:
                    found += scores(g - 1)
            found += scores(NG - 1)
            if l == 1:
                found += [("f", l, m) for m in range(FM // 2)]
            return found

        def readers(kind, l, i):
            return {"v": [("v", 2)], "s": [("q stack", i + 1), ("k stack", i + 1)], "m": [("max", i + 1)],
                    "e": [("probs", i + 1)], "r": [("reg probs", i + 1)], "f": [("hid", 2 * i + 2)],
                    "kr": [("kr f", NC)], "ks": [("kr stack", 1)], "vr": [("vr", 1)]}[kind]

        uses = []
        for l in range(LAYERS):
            if l == 1:
                uses += [("kr", 1, 0), ("ks", 1, 0), ("vr", 1, 0)]
            uses += ring_order(l)
        number = {use: n for n, use in enumerate(uses)}

        def slot(*use):
            return RING[number[use] % 2]

        loads = [("x", X, "xT"), ("vecs", VECS, "vecs"), ("gavg", GAVG, "gavg"), ("pcol", PCOL, "pcol"),
                 ("w0", WQKV[0], "w0"), ("relt", RELT, "relt"), ("hot", HOT, "hot"), ("abt", ABT, "abt"),
                 ("vb", VB, "vb"), ("bsel", BSEL, "bsel"), ("wo0", WO[0], "wo0"),
                 ("w2", WQKV[2], "w2"), ("regt", REGT, "regt"), ("mask", MASK, "mask"),
                 ("w1", WQKV[1], "w1"), ("wp", WP, "wp"), ("rope", ROPE, "rope"),
                 ("wo1", WO[1], "wo1"), ("ff1", W1, "ff1"), ("ff2", W2, "ff2"),
                 ("b1", B1, "b1"), ("wo2", WO[2], "wo2"), ("w3", WQKV[3], "w3"), ("wo3", WO[3], "wo3")]

        names = [f"{name} loaded" for name, _, _ in loads]
        names += ["ident", "backgrounds", "sel zero", "keys zero", "act chain", "dve chain", "pool chain",
                  "hot rows", "kr psum", "kr f", "kr parts", "ks psum", "kr stack", "vr psum", "vr", "ab cols",
                  "ab rows", "mask rows", "rel b0", "rel r", "rel b1", "rel b2", "sel", "idr",
                  "stored", "hid psum", "hid", "ff psum"]
        signals = {name: {l: count for l in range(LAYERS)} for name, count in {
            "stats": 2, "gstats": 1, "ve": 1, "y0": 1, "xn": 2, "q psum": 1, "k psum": 1, "v psum": 1, "qh": 1,
            "kh": 1, "ql": 1, "kl": 1, "spread": NU, "q stack": NU, "k stack": NU, "v": 2, "mt psum": NG, "mt": NG,
            "scores": NU, "probs": NU, "pv": NU, "u": NG, "d psum": NG, "rd": NG, "o": NG, "y psum": 1}.items()}
        signals |= {name: {l: 1 if l == 1 else NC for l in range(LAYERS)} for name in ("qf", "kf")}
        signals |= {name: {l: NG * PER[l] for l in range(LAYERS)} for name in ("max psum", "max")}
        signals |= {"x": {l: 3 * NC if l == 1 else NC for l in range(LAYERS)}}
        signals |= {name: {l: count for l in REL_LAYERS} for name, count in {
            "q b0": 1, "q r": 1, "q b1": 1, "q b2": 1, "rel psum": 2, "row f": 2, "col f": 2, "row h": 1, "col h": 1,
            "rel l": 2}.items()}
        signals |= {name: {t: count for t in (1, 3)} for name, count in {
            "ln mean": 1, "dev": 2, "sq": 2, "ln var psum": 1, "ln ve": 1, "ln y0": 1, "ln t": 2, "ni": 2}.items()}
        signals |= {name: {2: NG} for name in ("reg psum", "reg probs")}
        signals |= {name: {1: 0} for name in ("kr f", "kr stack", "vr", "hid")}
        names += [name for name in signals if name not in names]
        sems = {name: ctx.enter_context(nc.semaphore(name.replace(" ", "_"))) for name in names}

        def sem(name):
            return sems[name]

        def upto(name, l, count):
            return sems[name], sum(c for k, c in signals[name].items() if k < l) + count

        def loaded(eng, *what):
            for name in what:
                eng.wait_ge(sem(f"{name} loaded"), 16)

        def vec(name, i):
            return VECS[:, VEC[name] + i:VEC[name] + i + 1]

        block = ctx.enter_context(nc.Block())

        @block.sync
        def _(sync):
            for name, tile, src in loads:
                dst = tile[:, :, :] if len(tile.shape) == 3 else tile[:, :]
                sync.dma_start(dst, a[src]).then_inc(sem(f"{name} loaded"), 16)
            sync.wait_ge(*upto("x", 3, NC))
            sync.dma_start(out, X[:, :, :]).then_inc(sem("stored"), 16)
            sync.wait_ge(sem("stored"), 16)

        @block.gpsimd
        def _(pool):
            g = nc.gpsimd
            g.memset(IDF[:, :], 0.0).then_inc(sem("pool chain"), 1)
            pool.wait_ge(sem("pool chain"), 1)
            g.affine_select(out=IDF[:, :], in_=IDF[:, :], compare_op=ALU.not_equal, fill=1.0, base=0,
                            pattern=[[-1, P]], channel_multiplier=1).then_inc(sem("ident"), 1)
            pool.wait_ge(sem("ident"), 1)
            g.memset(KS[:, :, T:KW].bitcast(F32), 0.0).then_inc(sem("keys zero"), 1)
            pool.wait_ge(sem("keys zero"), 1)
            loaded(pool, "hot")
            g.tensor_copy(KS[64:128, :, 0:T], HOT[64:128, None, :].to_broadcast([64, NH, T]))\
                .then_inc(sem("hot rows"), 1)
            pool.wait_ge(sem("hot rows"), 1)
            for n, (tile, value) in enumerate((
                    (VX[:, :, :, :], 1.0), (NM[0][:, :, :].bitcast(F32), 0.0), (NM[1][:, :, :].bitcast(F32), 0.0),
                    (SELR[:, :, :], 0.0), (ONESC[:, :], 1.0 / C), (VR[:, :, :], 0.0),
                    (QS[1][96:128, :, :].bitcast(F32), 0.0))):
                g.memset(tile, value).then_inc(sem("backgrounds"), 1)
                pool.wait_ge(sem("backgrounds"), n + 1)
            pool.wait_ge(sem("ab cols"), 1)
            for h in range(NH):
                g.tensor_scalar(QS[1][64:96, h, :], HOT[64:96, :], ABS[64:96, 2, h:h + 1], ABS[64:96, 1, h:h + 1],
                                ALU.mult, ALU.add).then_inc(sem("ab rows"), 1)
                pool.wait_ge(sem("ab rows"), h + 1)
            loaded(pool, "mask")
            pool.wait_ge(*upto("scores", 0, NU))
            g.tensor_copy(QS[0][64:128, :, :], MASK[64:128, None, :].to_broadcast([64, NH, T]))\
                .then_inc(sem("mask rows"), 1)

        @block.scalar
        def _(act):
            n = [0]

            def link(ins):
                n[0] += 1
                ins.then_inc(sem("act chain"), 1)
                act.wait_ge(sem("act chain"), n[0])

            A = nc.scalar.activation

            def rel_parts():
                loaded(act, "relt")
                A(RELB[:, 0], RELT[:, :, :], ACT.Copy).then_inc(sem("rel b0"), 1)
                act.wait_ge(sem("rel r"), 1)
                A(RELB[:, 1], RELT[:, :, :], ACT.Copy).then_inc(sem("rel b1"), 1)

            def rsqrt_gn(l):
                act.wait_ge(*upto("ve", l, 1))
                link(A(GT[:, 1, :], GT[:, 0, :], ACT.Ln))
                A(GT[:, 2, :], GT[:, 1, :], ACT.Exp, scale=-0.5).then_inc(sem("y0"), 1)

            def layer_norm(t):
                for i in range(NC):
                    act.wait_ge(*upto("dev", t, i + 1))
                    A(SQ[:, i, :], DV[:, i, :], ACT.Square).then_inc(sem("sq"), 1)
                act.wait_ge(*upto("ln ve", t, 1))
                link(A(Y0[:, :], VE[:, :], ACT.Ln))
                A(Y0[:, :], Y0[:, :], ACT.Exp, scale=-0.5).then_inc(sem("ln y0"), 1)
                g, b = ("ln1g", "ln1b") if t == 1 else ("ln3g", "ln3b")
                for i in range(NC):
                    act.wait_ge(*upto("ln t", t, i + 1))
                    A(XN[:, i, :], SQ[:, i, :], ACT.Identity, bias=vec(b, i), scale=vec(g, i))\
                        .then_inc(sem("ni"), 1)

            def queries_keys(l):
                if l != 1:
                    act.wait_ge(*upto("q psum", l, 1))
                    for i in range(NC):
                        A(QF[:, i, :], PA[0:CC, i * T:(i + 1) * T], ACT.Identity, bias=vec(f"bq{l}", i))\
                            .then_inc(sem("qf"), 1)
                if l in REL_LAYERS:
                    act.wait_ge(*upto("qf", l, NC))
                    A(QB[:, 0], QF[:, :, :], ACT.Copy).then_inc(sem("q b0"), 1)
                    act.wait_ge(*upto("q r", l, 1))
                    A(QB[:, 1], QR[:, :, :], ACT.Copy).then_inc(sem("q b1"), 1)
                act.wait_ge(*upto("kf", l, NC if l != 1 else 1))
                A(KH[:, :, :], KF[:, :, :], ACT.Copy).then_inc(sem("kh"), 1)
                if l in REL_LAYERS:
                    act.wait_ge(*upto("rel psum", l, 1))
                    for i in range(NC):
                        A(RF[0][:, i, :].rearrange("p (r c) -> p r c", r=SIDE),
                          PC[0][0:CC, :].rearrange("p (r k c) -> p k r c", r=SIDE, k=NC)[:, i], ACT.Copy)\
                            .then_inc(sem("row f"), 1)
                    act.wait_ge(*upto("col f", l, NC))
                    A(RH[1][:, :, :], RF[1][:, :, :], ACT.Copy).then_inc(sem("col h"), 1)

            def q_stack(l, u):
                rows = P if l in REL_LAYERS else 64
                act.wait_ge(*upto("spread", l, u + 1))
                A(QS[l % 2][0:rows, 2 * u:2 * u + 2, :],
                  slot("s", l, u)[0:rows, 0, :].rearrange("p (h q) -> p h q", h=2), ACT.Copy)\
                    .then_inc(sem("q stack"), 1)

            def maxima(l, g):
                act.wait_ge(*upto("mt psum", l, g + 1))
                if g >= 2:
                    act.wait_ge(*upto("scores", l, 2 * (g - 1)))
                A(MT[g % 2][:, :], PA[:, 0:T], ACT.Copy).then_inc(sem("mt"), 1)

            def probs(l, u):
                act.wait_ge(*upto("scores", l, u + 1))
                if u >= 3:
                    act.wait_ge(*upto("pv", l, u - 2))
                A(PR[u % 3][:, :, :], slot("e", l, u)[:, :, :], ACT.Exp).then_inc(sem("probs"), 1)

            def reg_probs(l, g):
                act.wait_ge(*upto("reg psum", l, g + 1))
                if g >= 2:
                    act.wait_ge(*upto("pv", l, 2 * (g - 1)))
                A(PG[g % 2][:, :], slot("r", l, g)[:, 0, 0:T], ACT.Exp).then_inc(sem("reg probs"), 1)

            def recip(l, g):
                act.wait_ge(*upto("d psum", l, g + 1))
                if g >= 2:
                    act.wait_ge(*upto("o", l, g - 1))
                link(A(LD[g % 2][:, :], PC[g % 2][:, T:2 * T], ACT.Ln))
                A(RD[g % 2][:, :], LD[g % 2][:, :], ACT.Exp, scale=-1.0).then_inc(sem("rd"), 1)

            for l in range(LAYERS):
                rsqrt_gn(l)
                if l == 0:
                    rel_parts()
                if l == 1:
                    act.wait_ge(sem("kr psum"), 1)
                    for i in range(NC):
                        A(KRF[:, i, :], slot("kr", 1, 0)[0:CC, 0, i * NREG:(i + 1) * NREG], ACT.Identity,
                          bias=vec("bk2", i)).then_inc(sem("kr f"), 1)
                    layer_norm(1)
                queries_keys(l)
                for u in range(4):
                    q_stack(l, u)
                maxima(l, 0)
                if l == 2:
                    reg_probs(l, 0)
                probs(l, 0)
                probs(l, 1)
                q_stack(l, 4)
                q_stack(l, 5)
                maxima(l, 1)
                recip(l, 0)
                if l == 2:
                    reg_probs(l, 1)
                probs(l, 2)
                probs(l, 3)
                maxima(l, 2)
                recip(l, 1)
                if l == 2:
                    reg_probs(l, 2)
                probs(l, 4)
                probs(l, 5)
                recip(l, 2)
                if l == 1:
                    layer_norm(3)
                    loaded(act, "b1")
                    for m in range(FM):
                        act.wait_ge(sem("hid psum"), m // 2 + 1)
                        A(hidden(m), slot("f", 1, m // 2)[:, m % 2, 0:T], ACT.Gelu, bias=B1[:, m:m + 1])\
                            .then_inc(sem("hid"), 1)

        @block.vector
        def _(dve):
            n = [0]

            def link(ins):
                n[0] += 1
                ins.then_inc(sem("dve chain"), 1)
                dve.wait_ge(sem("dve chain"), n[0])

            V = nc.vector

            def selectors():
                V.memset(SEL[:, 0:4].bitcast(F32), 0.0).then_inc(sem("sel zero"), 1)
                V.memset(SEL[:, 4:8].bitcast(F32), 0.0).then_inc(sem("sel zero"), 1)
                dve.wait_ge(sem("ident"), 1)
                dve.wait_ge(sem("sel zero"), 2)
                for k, kind in enumerate(SEL_KINDS):
                    rows, scale = SEL_ROWS[kind]
                    order = "p (r c) -> p r c" if kind[0] in "qk" else "p (c r) -> p r c"
                    eye = IDF[0:CC, 0:CC].rearrange(order, r=HPC)
                    for row in rows:
                        V.tensor_scalar(SEL[:, k, :, row:row + HD], eye, scale, None, ALU.mult)\
                            .then_inc(sem("sel"), 1)
                V.tensor_copy(IDR[:, :], IDF[:, :]).then_inc(sem("idr"), 1)
                V.tensor_copy(SELM[:, :, :], IDF[:, 0:GH, None].to_broadcast([P, GH, P])).then_inc(sem("idr"), 1)
                dve.wait_ge(sem("backgrounds"), 7)
                V.tensor_copy(SELR[:, :, 0:NREG], IDF[:, 0:GH, None].to_broadcast([P, GH, NREG]))\
                    .then_inc(sem("idr"), 1)

            def rel_parts():
                dve.wait_ge(sem("rel b0"), 1)
                V.tensor_tensor(RELT[:, :, :], RELT[:, :, :], RELB[:, 0], ALU.subtract).then_inc(sem("rel r"), 1)
                dve.wait_ge(sem("rel b1"), 1)
                V.tensor_tensor(RELB[:, 2], RELT[:, :, :], RELB[:, 1], ALU.subtract).then_inc(sem("rel b2"), 1)

            def bias_cols():
                loaded(dve, "abt", "pcol")
                r = slice(64, 96)
                link(V.tensor_copy(ABH[r], ABT[r]))
                link(V.tensor_tensor(ABL[r], ABT[r], ABH[r].bitcast(F32), ALU.subtract))
                link(V.tensor_scalar(ABS[r, 0:2], ABH[r].bitcast(F32), PCOL[r, 0:1], None, ALU.mult))
                link(V.scalar_tensor_tensor(out=ABS[r, 0:2], in0=ABL[r], scalar=PCOL[r, 1:2], in1=ABS[r, 0:2],
                                            op0=ALU.mult, op1=ALU.add))
                V.tensor_tensor(ABS[r, 2], ABS[r, 0], ABS[r, 1], ALU.subtract).then_inc(sem("ab cols"), 1)

            def group_norm(l, dst):
                for i in range(NC):
                    link(V.bn_stats(STAT[:, i, :], X[:, i, :]))
                for i in range(NC):
                    link(V.bn_aggr(MS[:, i, :], STAT[:, i, :]))
                for i in range(NC):
                    V.scalar_tensor_tensor(out=MS[:, i, 1:2], in0=MS[:, i, 0:1], scalar=MS[:, i, 0:1],
                                           in1=MS[:, i, 1:2], op0=ALU.mult, op1=ALU.add)\
                        .then_inc(sem("stats"), 1)
                dve.wait_ge(*upto("gstats", l, 1))
                link(V.tensor_copy(GM[:, :, :], PA[0:CC, 0:2 * NC].rearrange("p (i s) -> p i s", i=NC)))
                link(V.tensor_tensor(GT[:, 3, :], GM[:, :, 0], GM[:, :, 0], ALU.mult))
                V.scalar_tensor_tensor(out=GT[:, 0, :], in0=GM[:, :, 1], scalar=GN_EPS, in1=GT[:, 3, :],
                                       op0=ALU.add, op1=ALU.subtract).then_inc(sem("ve"), 1)
                dve.wait_ge(*upto("y0", l, 1))
                link(V.tensor_tensor(GT[:, 3, :], GT[:, 2, :], GT[:, 2, :], ALU.mult))
                link(V.scalar_tensor_tensor(out=GT[:, 4, :], in0=GT[:, 3, :], scalar=-0.5, in1=GT[:, 0, :],
                                            op0=ALU.mult, op1=ALU.mult))
                link(V.scalar_tensor_tensor(out=GT[:, 5, :], in0=GT[:, 4, :], scalar=1.5, in1=GT[:, 2, :],
                                            op0=ALU.add, op1=ALU.mult))
                for i in range(NC):
                    V.tensor_scalar(dst[:, i, :], X[:, i, :], GM[:, i, 0:1], GT[:, 5, i:i + 1],
                                    ALU.subtract, ALU.mult).then_inc(sem("xn"), 1)

            def layer_norm(t):
                dve.wait_ge(*upto("ln mean", t, 1))
                for i in range(NC):
                    V.tensor_tensor(DV[:, i, :], FL[:, i, :], PA[0:CC, 0:T], ALU.subtract)\
                        .then_inc(sem("dev"), 1)
                dve.wait_ge(*upto("ln var psum", t, 1))
                V.tensor_scalar(VE[:, :], PB[0:CC, 0:T], LN_EPS, None, ALU.add).then_inc(sem("ln ve"), 1)
                dve.wait_ge(*upto("ln y0", t, 1))
                link(V.tensor_tensor(YN[:, :], Y0[:, :], Y0[:, :], ALU.mult))
                link(V.scalar_tensor_tensor(out=YN[:, :], in0=YN[:, :], scalar=-0.5, in1=VE[:, :],
                                            op0=ALU.mult, op1=ALU.mult))
                link(V.scalar_tensor_tensor(out=YN[:, :], in0=YN[:, :], scalar=1.5, in1=Y0[:, :],
                                            op0=ALU.add, op1=ALU.mult))
                for i in range(NC):
                    V.tensor_tensor(SQ[:, i, :], DV[:, i, :], YN[:, :], ALU.mult).then_inc(sem("ln t"), 1)

            def hi_lo(src, hi, lo, src_ready, hi_signal, hi_ready, lo_signal):
                dve.wait_ge(*src_ready)
                V.tensor_copy(hi, src).then_inc(sem(hi_signal), 1)
                dve.wait_ge(*hi_ready)
                V.tensor_tensor(lo, src, hi.bitcast(F32), ALU.subtract).then_inc(sem(lo_signal), 1)

            def rotate(l, dst, plain, swapped, b, bp, ready, done):
                dve.wait_ge(*upto(ready, l, 1))
                for i in range(NC):
                    V.scalar_tensor_tensor(out=RF[0][:, i, :], in0=plain[0:CC, i * T:(i + 1) * T], scalar=vec(b, i),
                                           in1=ROPE[:, 0, :], op0=ALU.add, op1=ALU.mult)\
                        .then_inc(sem("dve chain"), 1)
                    V.scalar_tensor_tensor(out=RF[1][:, i, :], in0=swapped[0:CC, i * T:(i + 1) * T],
                                           scalar=vec(bp, i), in1=ROPE[:, 1, :], op0=ALU.add, op1=ALU.mult)\
                        .then_inc(sem("dve chain"), 1)
                n[0] += 2 * NC
                dve.wait_ge(sem("dve chain"), n[0])
                V.tensor_tensor(dst[:, :, :], RF[0][:, :, :], RF[1][:, :, :], ALU.add).then_inc(sem(done), 1)

            def queries_keys(l):
                if l == 1:
                    loaded(dve, "rope")
                    rotate(l, QF, PA, PC[0], "bq1", "bqp", "q psum", "qf")
                    hi_lo(QF[:, :, :], QH[:, :, :], QL[:, :, :], upto("qf", 1, 1), "qh", upto("qh", 1, 1), "ql")
                    rotate(l, KF, PB, PC[1], "bk1", "bkp", "k psum", "kf")
                else:
                    dve.wait_ge(*upto("k psum", l, 1))
                    for i in range(NC):
                        V.tensor_scalar(KF[:, i, :], PB[0:CC, i * T:(i + 1) * T], vec(f"bk{l}", i), None, ALU.add)\
                            .then_inc(sem("kf"), 1)
                    if l in REL_LAYERS:
                        dve.wait_ge(*upto("q b0", l, 1))
                        V.tensor_tensor(QR[:, :, :], QF[:, :, :], QB[:, 0], ALU.subtract).then_inc(sem("q r"), 1)
                    hi_lo(QF[:, :, :], QH[:, :, :], QL[:, :, :], upto("qf", l, NC), "qh", upto("qh", l, 1), "ql")
                    if l in REL_LAYERS:
                        dve.wait_ge(*upto("q b1", l, 1))
                        V.tensor_tensor(QB[:, 2], QR[:, :, :], QB[:, 1], ALU.subtract).then_inc(sem("q b2"), 1)
                dve.wait_ge(*upto("kh", l, 1))
                V.tensor_tensor(KL[:, :, :], KF[:, :, :], KH[:, :, :].bitcast(F32), ALU.subtract)\
                    .then_inc(sem("kl"), 1)
                dve.wait_ge(*upto("v psum", l, 1))
                if l == 0:
                    dve.wait_ge(sem("backgrounds"), 7)
                    loaded(dve, "vb")
                for c in range(2):
                    V.tensor_tensor(VX[:, c, :, 0:HD],
                                    slot("v", l, 0)[:, 0, c * C:(c + 1) * C].rearrange("p (h d) -> p h d", h=NH),
                                    VB[:, l, :].rearrange("p (h d) -> p h d", h=NH), ALU.add)\
                        .then_inc(sem("v"), 1)
                if l in REL_LAYERS:
                    dve.wait_ge(*upto("rel psum", l, 2))
                    for i in range(NC):
                        V.tensor_copy(RF[1][:, i, :].rearrange("p (r c) -> p r c", r=SIDE),
                                      PC[1][0:CC, :].rearrange("p (c k r) -> p k r c", c=SIDE, k=NC)[:, i])\
                            .then_inc(sem("col f"), 1)
                    hi_lo(RF[0][:, :, :], RH[0][:, :, :], RL[0][:, :, :], upto("row f", l, NC), "row h",
                          upto("row h", l, 1), "rel l")
                    dve.wait_ge(*upto("col h", l, 1))
                    V.tensor_tensor(RL[1][:, :, :], RF[1][:, :, :], RH[1][:, :, :].bitcast(F32), ALU.subtract)\
                        .then_inc(sem("rel l"), 1)

            def k_stack(l, u):
                dve.wait_ge(*upto("spread", l, u + 1))
                V.tensor_copy(KS[0:64, 2 * u:2 * u + 2, 0:T],
                              slot("s", l, u)[0:64, 1, :].rearrange("p (h k) -> p h k", h=2))\
                    .then_inc(sem("k stack"), 1)

            def maxima(l, g):
                if g >= 2:
                    dve.wait_ge(*upto("mt psum", l, g - 1))
                for i in range(PER[l]):
                    m = PER[l] * g + i
                    dve.wait_ge(*upto("max psum", l, m + 1))
                    if l == 2:
                        V.tensor_reduce(NM[g % 2][:, :, i], slot("m", l, m)[:, :, 0:T + NREG], AX.X, ALU.max,
                                        negate=True).then_inc(sem("max"), 1)
                    else:
                        V.tensor_reduce(NM[g % 2][:, :, 2 * i:2 * i + 2].rearrange("p q j -> p j q"),
                                        slot("m", l, m)[:, :, :].rearrange("p j (q k) -> p j q k", q=2),
                                        AX.X, ALU.max, negate=True).then_inc(sem("max"), 1)

            def unnormalised(l, g):
                dve.wait_ge(*upto("pv", l, 2 * g + 2))
                if g >= 2:
                    dve.wait_ge(*upto("o", l, g - 1))
                V.tensor_copy(U[g % 2][:, :], PC[g % 2][:, 0:T]).then_inc(sem("u"), 1)

            def normalised(l, g):
                dve.wait_ge(*upto("rd", l, g + 1))
                link(V.scalar_tensor_tensor(out=LD[g % 2][:, :], in0=PC[g % 2][:, T:2 * T], scalar=-1.0,
                                            in1=RD[g % 2][:, :], op0=ALU.mult, op1=ALU.mult))
                link(V.scalar_tensor_tensor(out=LD[g % 2][:, :], in0=LD[g % 2][:, :], scalar=2.0,
                                            in1=RD[g % 2][:, :], op0=ALU.add, op1=ALU.mult))
                V.tensor_tensor(O[g][:, :], LD[g % 2][:, :], U[g % 2][:, :], ALU.mult).then_inc(sem("o"), 1)

            def registers():
                hi_lo(KRF[:, :, :], KRH[:, :, :], KRL[:, :, :], (sem("kr f"), NC), "kr parts", (sem("kr parts"), 1),
                      "kr parts")
                dve.wait_ge(sem("ks psum"), 1)
                dve.wait_ge(sem("keys zero"), 1)
                V.tensor_copy(KS[0:64, :, T:T + NREG],
                              slot("ks", 1, 0)[0:64, 0, 0:NH * NREG].rearrange("p (h k) -> p h k", h=NH))\
                    .then_inc(sem("kr stack"), 1)
                dve.wait_ge(sem("vr psum"), 1)
                V.tensor_tensor(VRB[:, :], slot("vr", 1, 0)[:, 0, 0:C], VB[:, 2, :], ALU.add).then_inc(sem("vr"), 1)
                dve.wait_ge(sem("vr"), 1)
                for j in range(GH):
                    q = slice(32 * j, 32 * j + 32)
                    V.tensor_scalar(VR[q, j:NH:GH, 0:HD],
                                    VRB[q, :].rearrange("p (h d) -> p h d", h=NH)[:, j:NH:GH], PCOL[q, 2:3], None,
                                    ALU.mult).then_inc(sem("vr"), 1)
                    V.tensor_copy(VR[q, j:NH:GH, HD:32], PCOL[q, 2:3, None].to_broadcast([32, NG, HD]))\
                        .then_inc(sem("vr"), 1)

            loaded(dve, "x")
            for l in range(LAYERS):
                group_norm(l, FL if l == 1 else XN)
                if l == 0:
                    loaded(dve, "vecs")
                    selectors()
                    rel_parts()
                    bias_cols()
                if l == 1:
                    registers()
                    layer_norm(1)
                queries_keys(l)
                for u in range(2):
                    k_stack(l, u)
                maxima(l, 0)
                for u in range(2, 4):
                    k_stack(l, u)
                maxima(l, 1)
                for u in range(4, 6):
                    k_stack(l, u)
                unnormalised(l, 0)
                maxima(l, 2)
                normalised(l, 0)
                for g in range(1, NG):
                    unnormalised(l, g)
                    normalised(l, g)
                dve.wait_ge(*upto("y psum", l, 1))
                if l != 1:
                    for i in range(NC):
                        ins = V.scalar_tensor_tensor(out=X[:, i, :], in0=PB[0:CC, i * T:(i + 1) * T],
                                                     scalar=vec(f"bo{l}", i), in1=X[:, i, :],
                                                     op0=ALU.add, op1=ALU.add)
                        ins.then_inc(sem("x"), 1)
                else:
                    for i in range(NC):
                        V.scalar_tensor_tensor(out=FL[:, i, :], in0=PB[0:CC, i * T:(i + 1) * T],
                                               scalar=vec("bo1", i), in1=FL[:, i, :],
                                               op0=ALU.add, op1=ALU.add).then_inc(sem("x"), 1)
                    dve.wait_ge(*upto("x", 1, NC))
                    layer_norm(3)
                    dve.wait_ge(sem("ff psum"), 1)
                    for i in range(NC):
                        V.scalar_tensor_tensor(out=FL[:, i, :], in0=PA[0:CC, i * T:(i + 1) * T],
                                               scalar=vec("b2", i), in1=FL[:, i, :],
                                               op0=ALU.add, op1=ALU.add).then_inc(sem("x"), 1)
                    dve.wait_ge(*upto("x", 1, 2 * NC))
                    for i in range(NC):
                        V.tensor_tensor(X[:, i, :], X[:, i, :], FL[:, i, :], ALU.add).then_inc(sem("x"), 1)
                dve.wait_ge(*upto("x", l, 3 * NC if l == 1 else NC))

        @block.tensor
        def _(pe):
            M = nc.tensor.matmul

            def take(*use):
                if number[use] >= 2:
                    former = uses[number[use] - 2]
                    for name, count in readers(*former):
                        pe.wait_ge(*upto(name, former[1], count))
                return slot(*use)

            def project(psum, w, c0, src, ready, n_ready):
                for m in range(NC):
                    for k in range(NC):
                        pe.wait_ge(ready, n_ready)
                        ins = M(psum[0:CC, m * T:(m + 1) * T], w[:, k, c0 + m * CC:c0 + (m + 1) * CC], src[:, k, :],
                                start=(k == 0), stop=(k == NC - 1))
                return ins

            def relative(l):
                pe.wait_ge(sem("rel b1"), 1)
                pe.wait_ge(sem("rel b2"), 1)
                pe.wait_ge(*upto("q b1", l, 1))
                pe.wait_ge(*upto("q b2", l, 1))
                for w in range(2):
                    table = 2 * REL_LAYERS.index(l) + w
                    for i in range(SIDE):
                        at = slice(i * SIDE, (i + 1) * SIDE) if w == 0 else slice(i, T, SIDE)
                        for t, (tp, qp) in enumerate(TERMS):
                            lhsT = RELB[:, tp, table, (SIDE - 1 - i) * HPC:(NREL - i) * HPC]
                            ins = M(PC[w][0:CC, i * 2 * SIDE:(i + 1) * 2 * SIDE].rearrange("p (k c) -> p k c", k=NC),
                                    lhsT, QB[:, qp, :, at], start=(t == 0), stop=(t == len(TERMS) - 1))
                    ins.then_inc(sem("rel psum"), 1)

            def spread(l, u):
                s = take("s", l, u)
                if u == 0:
                    for name in ("qh", "ql", "kh", "kl"):
                        pe.wait_ge(*upto(name, l, 1))
                    if l in REL_LAYERS:
                        for name, count in (("row h", 1), ("col h", 1), ("rel l", 2)):
                            pe.wait_ge(*upto(name, l, count))
                    if l == 0:
                        pe.wait_ge(sem("sel"), sum(len(SEL_ROWS[k][0]) for k in SEL_KINDS))
                for bank, parts in enumerate(((("qh", QH), ("ql", QL)), (("kh", KH), ("kl", KL)))):
                    if bank == 0 and l in REL_LAYERS:
                        parts += (("rh", RH[0]), ("rl", RL[0]), ("ch", RH[1]), ("cl", RL[1]))
                    for i in range(2):
                        h = 2 * u + i
                        for t, (kind, src) in enumerate(parts):
                            ins = M(s[:, bank, i * T:(i + 1) * T], SEL[:, SEL_KINDS.index(kind), h % HPC, :],
                                    src[:, h // HPC, :], start=(t == 0), stop=(t == len(parts) - 1))
                ins.then_inc(sem("spread"), 1)

            def for_maxima(l, g):
                for i in range(PER[l]):
                    m = PER[l] * g + i
                    s = take("m", l, m)
                    heads = 2 if PER[l] == 2 else 1
                    u = (heads * m) // 2
                    pe.wait_ge(*upto("q stack", l, u + 1))
                    pe.wait_ge(*upto("k stack", l, u + 1))
                    for k in range(heads):
                        h = heads * m + k
                        for q in range(2):
                            dst = s[:, k, q * T:(q + 1) * T] if heads == 2 else s[:, q, 0:T + NREG]
                            ins = M(dst, QS[l % 2][:, h, q * P:(q + 1) * P], KS[:, h, 0:dst.shape[1]],
                                    start=True, stop=True)
                    ins.then_inc(sem("max psum"), 1)

            def turn_maxima(l, g):
                pe.wait_ge(*upto("max", l, PER[l] * (g + 1)))
                if g == 0:
                    pe.wait_ge(sem("idr"), 3)
                else:
                    pe.wait_ge(*upto("mt", l, g))
                for q in range(2):
                    ins = M(PA[:, q * P:(q + 1) * P], NM[g % 2][:, q, :], IDR[:, :], start=True, stop=True)
                ins.then_inc(sem("mt psum"), 1)

            def reg_scores(l, g):
                s = take("r", l, g)
                pe.wait_ge(*upto("mt", l, g + 1))
                for j in range(GH):
                    dst = s[32 * j:32 * j + 32, 0, 0:T]
                    M(dst, KS[:, GH * g + j, T:KW].bitcast(F32), QS[l % 2][:, GH * g + j, :].bitcast(F32),
                      start=True, stop=False)
                    ins = M(dst, SELR[:, j, :], MT[g % 2][:, :].bitcast(F32), start=False, stop=True)
                ins.then_inc(sem("reg psum"), 1)

            def scores(l, u):
                s = take("e", l, u)
                pe.wait_ge(*upto("mt", l, u // 2 + 1))
                for i in range(2):
                    h = 2 * u + i
                    for k in range(2):
                        dst = s[:, i, k * T:(k + 1) * T]
                        M(dst, KS[:, h, k * P:(k + 1) * P], QS[l % 2][:, h, :], start=True, stop=False)
                        ins = M(dst, SELM[:, h % GH, :], MT[u // 2 % 2][:, :], start=False, stop=True)
                ins.then_inc(sem("scores"), 1)

            def values(l, u):
                g = u // 2
                pe.wait_ge(*upto("probs", l, u + 1))
                if u == 0:
                    pe.wait_ge(*upto("v", l, 2))
                if u == 0 and l == 2:
                    pe.wait_ge(sem("vr"), 1 + 2 * GH)
                if u % 2 == 0 and g >= 2:
                    pe.wait_ge(*upto("o", l, g - 1))
                if l == 2:
                    pe.wait_ge(*upto("reg probs", l, g + 1))
                for i in range(2):
                    h = 2 * u + i
                    q = 32 * (h % GH)
                    dst = PC[g % 2][q:q + 32, 0:T]
                    for k in range(2):
                        ins = M(dst, VX[:, k, h, :], PR[u % 3][:, i, k * T:(k + 1) * T], start=(k == 0),
                                stop=(k == 1 and l != 2))
                    if l == 2:
                        ins = M(dst, VR[:, h, :], PG[g % 2][:, :], start=False, stop=True)
                ins.then_inc(sem("pv"), 1)

            def row_sums(l, g):
                if l == 0 and g == 0:
                    loaded(pe, "bsel")
                pe.wait_ge(*upto("u", l, g + 1))
                M(PC[g % 2][:, T:2 * T], BSEL[:, :], U[g % 2][:, :], start=True, stop=True)\
                    .then_inc(sem("d psum"), 1)

            def out_project(l, g):
                if g == 0:
                    loaded(pe, f"wo{l}")
                pe.wait_ge(*upto("o", l, g + 1))
                for m in range(NC):
                    ins = M(PB[0:CC, m * T:(m + 1) * T], WO[l][:, g, m * CC:(m + 1) * CC], O[g][:, :],
                            start=(g == 0 and m == 0), stop=(g == NG - 1), skip_group_check=True)
                if g == NG - 1:
                    ins.then_inc(sem("y psum"), 1)

            def registers():
                s = take("kr", 1, 0)
                loaded(pe, "w2", "regt")
                for m in range(NC):
                    for k in range(NC):
                        ins = M(s[0:CC, 0, m * NREG:(m + 1) * NREG], WQKV[2][:, k, C + m * CC:C + (m + 1) * CC],
                                REGT[:, k, 0:NREG], start=(k == 0), stop=(k == NC - 1))
                ins.then_inc(sem("kr psum"), 1)
                s = take("ks", 1, 0)
                pe.wait_ge(sem("kr parts"), 2)
                for h in range(NH):
                    for t, (kind, src) in enumerate((("kh", KRH), ("kl", KRL))):
                        ins = M(s[:, 0, h * NREG:(h + 1) * NREG], SEL[:, SEL_KINDS.index(kind), h % HPC, :],
                                src[:, h // HPC, :], start=(t == 0), stop=(t == 1))
                ins.then_inc(sem("ks psum"), 1)
                s = take("vr", 1, 0)
                for k in range(NC):
                    ins = M(s[:, 0, 0:C], REGT[:, k, :], WQKV[2][:, k, 2 * C:3 * C], start=(k == 0),
                            stop=(k == NC - 1))
                ins.then_inc(sem("vr psum"), 1)

            def layer_norm(t, ready, n_ready):
                pe.wait_ge(ready, n_ready)
                for k in range(NC):
                    ins = M(PA[0:CC, 0:T], ONESC[:, :], FL[:, k, :], start=(k == 0), stop=(k == NC - 1))
                ins.then_inc(sem("ln mean"), 1)
                for k in range(NC):
                    pe.wait_ge(*upto("sq", t, k + 1))
                    ins = M(PB[0:CC, 0:T], ONESC[:, :], SQ[:, k, :], start=(k == 0), stop=(k == NC - 1))
                ins.then_inc(sem("ln var psum"), 1)

            for l in range(LAYERS):
                if l == 0:
                    loaded(pe, "gavg")
                pe.wait_ge(*upto("stats", l, NC))
                M(PA[0:CC, 0:2 * NC], GAVG[:, :], MS[:, :, :], start=True, stop=True)\
                    .then_inc(sem("gstats"), 1)
                ready = upto("xn", l, NC)
                if l == 1:
                    registers()
                    pe.wait_ge(sem("backgrounds"), 7)
                    layer_norm(1, *ready)
                    ready = upto("ni", 1, NC)
                loaded(pe, f"w{l}")
                last = project(PA, WQKV[l], 0, XN, *ready)
                if l == 1:
                    loaded(pe, "wp")
                    last = project(PC[0], WP, 0, XN, *ready)
                last.then_inc(sem("q psum"), 1)
                last = project(PB, WQKV[l], C, XN, *ready)
                if l == 1:
                    last = project(PC[1], WP, C, XN, *ready)
                last.then_inc(sem("k psum"), 1)
                s = take("v", l, 0)
                for c in range(2):
                    for k in range(NC):
                        ins = M(s[:, 0, c * C:(c + 1) * C], XN[:, k, c * P:(c + 1) * P],
                                WQKV[l][:, k, 2 * C:3 * C], start=(k == 0), stop=(k == NC - 1))
                ins.then_inc(sem("v psum"), 1)
                if l in REL_LAYERS:
                    relative(l)

                spread(l, 0)
                spread(l, 1)
                if l == 0:
                    pe.wait_ge(sem("hot rows"), 1)
                if l == 1:
                    pe.wait_ge(sem("ab rows"), NH)
                if l == 2:
                    pe.wait_ge(sem("mask rows"), 1)
                for_maxima(l, 0)
                spread(l, 2)
                spread(l, 3)
                turn_maxima(l, 0)
                for_maxima(l, 1)
                if l == 2:
                    reg_scores(l, 0)
                scores(l, 0)
                scores(l, 1)
                values(l, 0)
                spread(l, 4)
                spread(l, 5)
                turn_maxima(l, 1)
                values(l, 1)
                for_maxima(l, 2)
                row_sums(l, 0)
                if l == 2:
                    reg_scores(l, 1)
                scores(l, 2)
                scores(l, 3)
                values(l, 2)
                turn_maxima(l, 2)
                values(l, 3)
                row_sums(l, 1)
                out_project(l, 0)
                if l == 2:
                    reg_scores(l, 2)
                scores(l, 4)
                scores(l, 5)
                values(l, 4)
                out_project(l, 1)
                values(l, 5)
                row_sums(l, 2)
                out_project(l, 2)
                if l == 1:
                    layer_norm(3, *upto("x", 1, NC))
                    loaded(pe, "ff1", "ff2")
                    pe.wait_ge(*upto("ni", 3, NC))
                    for m in range(FM // 2):
                        s = take("f", 1, m)
                        for i in range(2):
                            for k in range(NC):
                                c = 2 * m + i
                                ins = M(s[:, i, 0:T], W1[:, k, c * P:(c + 1) * P], XN[:, k, :], start=(k == 0),
                                        stop=(k == NC - 1))
                        ins.then_inc(sem("hid psum"), 1)
                    for c in range(FM):
                        pe.wait_ge(sem("hid"), c + 1)
                        for m in range(NC):
                            ins = M(PA[0:CC, m * T:(m + 1) * T], W2[:, c, m * CC:(m + 1) * CC], hidden(c),
                                    start=(c == 0 and m == 0), stop=(c == FM - 1), skip_group_check=True)
                    ins.then_inc(sem("ff psum"), 1)


def layouts(inp):
    f32 = np.float32
    heads = np.arange(NH)

    def chunks(w):
        return np.ascontiguousarray(w.reshape(NC, CC, -1).transpose(1, 0, 2))

    def column(v):
        return v.reshape(NC, CC).T

    def by_quadrant(w):
        padded = np.zeros((NG, GH, 32, C), f32)
        padded[:, :, :HD] = w.reshape(NG, GH, HD, C)
        return np.ascontiguousarray(padded.transpose(1, 2, 0, 3).reshape(P, NG, C))

    def swapped(w):
        return w.reshape(*w.shape[:-1], NH, 2, HD // 2)[..., ::-1, :].reshape(w.shape)

    def toeplitz(rel):
        t = np.zeros((HPC, HD, 32, HPC), f32)
        for r in range(HPC):
            t[r, :, :NREL, r] = rel[:NREL][::-1].T
        return t.reshape(CC, HPC * 32)

    L = {k: np.asarray(v) for k, v in inp.items()}
    wqkv = [L["L0_conv_qkv_w"], np.concatenate([L["L1_conv_wq"], L["L1_conv_wk"], L["L1_conv_wv"]], 1),
            L["L2_conv_qkv_w"].T, L["L3_conv_qkv_w"].T]
    bqkv = [L["L0_conv_qkv_b"], np.concatenate([L["L1_conv_bq"], L["L1_conv_bk"], L["L1_conv_bv"]]),
            L["L2_conv_qkv_b"], L["L3_conv_qkv_b"]]
    wo = [L["L0_conv_proj_w"], L["L1_conv_wo"], L["L2_conv_out_w"].T, L["L3_conv_proj_w"].T]
    bo = [L["L0_conv_proj_b"], L["L1_conv_bo"], L["L2_conv_out_b"], L["L3_conv_proj_b"]]

    vecs = np.zeros((CC, 2 * len(VEC)), f32)
    named = {f"b{v}{l}": (bqkv[l][n * C:(n + 1) * C]) for l in range(LAYERS) for n, v in enumerate("qk")}
    named |= {f"bo{l}": bo[l] for l in range(LAYERS)}
    named |= {"bqp": swapped(L["L1_conv_bq"]), "bkp": swapped(L["L1_conv_bk"]), "ln1g": L["L1_conv_ln1_g"],
              "ln1b": L["L1_conv_ln1_b"], "ln3g": L["L1_conv_ln3_g"], "ln3b": L["L1_conv_ln3_b"],
              "b2": L["L1_conv_b2"]}
    for name, v in named.items():
        vecs[:, VEC[name]:VEC[name] + NC] = column(v)

    place = np.arange(T)
    row, col, k = place // SIDE, place % SIDE, np.arange(SIDE)[:, None]
    hot = np.zeros((P, T), f32)
    hot[64:80] = hot[80:96] = row == k
    hot[96:112] = hot[112:128] = col == k
    first = np.clip(np.arange(SIDE) - 3, 0, SIDE - 7)
    mask = np.zeros((P, T), f32)
    mask[64:80] = np.where((k >= first[row]) & (k < first[row] + 7), 0, MASKED)
    mask[96:112] = np.where((k >= first[col]) & (k < first[col] + 7), 0, MASKED)
    angles = HD // 4
    timescale = np.concatenate([f32(10000.0) ** (f32(2) * np.arange(angles, dtype=f32) / f32(HD)),
                                np.full(HD // 2 - angles, np.inf, f32)]).astype(f32)
    angle = (place.astype(f32)[:, None] / timescale).astype(f32)
    sin, cos = np.sin(angle).T, np.cos(angle).T
    rope = np.stack([np.tile(np.concatenate([cos, cos]), (HPC, 1)), np.tile(np.concatenate([-sin, sin]), (HPC, 1))], 1)
    group = np.arange(CC) // GN_GROUP
    pcol = np.zeros((P, 3), f32)
    pcol[64:80, 0] = 1
    pcol[80:96, 1] = 1
    pcol[:, 2] = np.arange(P) % 32 < NREG
    bsel = np.zeros((P, P), f32)
    for j in range(GH):
        bsel[32 * j + HD, 32 * j:32 * j + 32] = 1
    abt = np.zeros((P, 2, NH), f32)
    abt[64:96] = L["L1_conv_attn_biases"].T
    regt = np.zeros((CC, NC, GH, 32), f32)
    regt[:, :, :, :NREG] = chunks(L["L2_conv_registers"].T)[:, :, None, :]

    arrays = {"xT": chunks(L["x"].reshape(T, C).T), "vecs": vecs, "gavg": (group[:, None] == group) / f32(GN_GROUP),
              "pcol": pcol, "relt": np.stack([toeplitz(L[f"L{l}_conv_rel_pos_{v}"]) for l in REL_LAYERS for v in "hw"], 1),
              "hot": hot, "mask": mask, "abt": abt, "bsel": bsel, "rope": rope, "regt": regt.reshape(CC, NC, P),
              "vb": np.broadcast_to(np.stack([b[2 * C:] for b in bqkv]), (P, LAYERS, C)),
              "wp": chunks(np.concatenate([swapped(L["L1_conv_wq"]), swapped(L["L1_conv_wk"])], 1)),
              "ff1": chunks(L["L1_conv_w1"]), "ff2": L["L1_conv_w2"].reshape(FM, P, C).transpose(1, 0, 2),
              "b1": L["L1_conv_b1"].reshape(FM, P).T}
    for l in range(LAYERS):
        arrays[f"w{l}"] = chunks(wqkv[l])
        arrays[f"wo{l}"] = by_quadrant(wo[l])
    return {name: np.ascontiguousarray(v, dtype=f32) for name, v in arrays.items()}


def kernel(**inputs):
    import concourse.bacc as bacc
    from concourse.bass_utils import run_bass_kernel_spmd

    nc = bacc.Bacc("TRN2", target_bir_lowering=False, num_devices=1)
    arrays = layouts(inputs)
    args = {name: nc.dram_tensor(f"in_{name}", v.shape, F32, kind="ExternalInput").ap() for name, v in arrays.items()}
    out = nc.dram_tensor("out_xT", (CC, NC, T), F32, kind="ExternalOutput").ap()
    build(nc, args, out)
    r = run_bass_kernel_spmd(nc, [{f"in_{name}": v for name, v in arrays.items()}], core_ids=[0])
    got = r.results[0]["out_xT"]
    return got.transpose(2, 1, 0).reshape(1, SIDE, SIDE, C)
```

```python
from contextlib import ExitStack

import numpy as np

import concourse.bass as bass
from concourse import mybir
from concourse.alu_op_type import AluOpType as ALU

ACT = mybir.ActivationFunctionType
AX = mybir.AxisListType
F32 = mybir.dt.float32
F32R = mybir.dt.float32r
BF16 = mybir.dt.bfloat16

SIDE = 16
T = SIDE * SIDE
C = 192
CC = 96
NC = C // CC
HD = 16
NH = C // HD
HPC = CC // HD
P = 128
NG = 3
GH = 4
NU = NH // 2
NREG = 16
FF = 768
FM = FF // P
KEY0 = NREG
REG1 = KEY0 + T
KW = REG1 + 32
WINDOW = NREG + (SIDE // 2 + 3) * SIDE
GN_GROUP = C // 32
GN_EPS = 1e-5
LN_EPS = 1e-5
NREL = 2 * SIDE - 1
QK_SCALE = HD ** -0.5
MASKED = -2.0 ** 100
LAYERS = 4
REL_LAYERS = (0, 3)
TERMS = ((0, 0), (0, 1), (1, 0), (0, 2), (1, 1), (2, 0))

VEC = {name: 2 * n for n, name in enumerate(
    [f"bk{l}" for l in range(LAYERS)] + ["bkp"]
    + [f"{v}{l}" for l in range(LAYERS) for v in ("bq", "bo")] + ["bqp", "ln1g", "ln1b", "ln3g", "ln3b", "b2"])}

SCALED = ("w0", "w2", "w1", "wp", "w3")

REL_ROWS = {"row h": 64, "row l": 80, "col h": 96, "col l": 112}


def build(nc, a, out):
    with ExitStack() as ctx:
        def sb(name, shape, dt=F32):
            return ctx.enter_context(nc.sbuf_tensor(name, shape, dt))

        def ps(name, shape):
            return ctx.enter_context(nc.psum_tensor(name, shape, F32))

        X = sb("X", [CC, NC, T])
        XN = sb("XN", [CC, NC, T])
        FL = sb("FL", [CC, NC, T])
        DV = sb("DV", [CC, NC, T])
        SQ = sb("SQ", [CC, NC, T])
        VE = sb("VE", [CC, T])
        Y0 = sb("Y0", [CC, T])
        YN = sb("YN", [CC, T])
        QF = sb("QF", [CC, NC, T])
        KF = sb("KF", [CC, NC, T])
        QH = sb("QH", [CC, NC, T], F32R)
        QL = sb("QL", [CC, NC, T], F32R)
        KH = sb("KH", [CC, NC, T], F32R)
        KL = sb("KL", [CC, NC, T], F32R)
        QB = sb("QB", [CC, 3, NC, T], BF16)
        QC = sb("QC", [CC, 3 * NC, SIDE, SIDE], BF16)
        QR = sb("QR", [CC, NC, T])
        RF = [sb(f"RF{i}", [CC, NC, T]) for i in range(2)]
        RH = [sb(f"RH{i}", [CC, NC, T], F32R) for i in range(2)]
        RL = [sb(f"RL{i}", [CC, NC, T], F32R) for i in range(2)]
        QS = [sb(f"QS{i}", [P, NH, T], F32R) for i in range(2)]
        KS = sb("KS", [P, NH, KW], F32R)
        VX = sb("VX", [P, 2, NH, 32])
        VR = sb("VR", [P, NH, 32])
        PR = [sb(f"PR{i}", [P, 2, 2 * T]) for i in range(3)]
        PG = [sb(f"PG{i}", [P, T]) for i in range(2)]
        NM = [sb(f"NM{i}", [P, 2, P], F32R) for i in range(2)]
        MT = [sb(f"MT{i}", [P, T], F32R) for i in range(2)]
        U = [sb(f"U{i}", [P, T]) for i in range(2)]
        LD = [sb(f"LD{i}", [P, T]) for i in range(2)]
        RD = [sb(f"RD{i}", [P, T]) for i in range(2)]
        O = [sb(f"O{i}", [P, T]) for i in range(NG)]
        STAT = sb("STAT", [CC, NC, 6])
        MS = sb("MS", [CC, NC, 2])
        GM = sb("GM", [CC, NC, 2])
        GT = sb("GT", [CC, 6, NC])

        WQKV = [sb(f"WQKV{l}", [CC, NC, 3 * C]) for l in range(LAYERS)]
        WP = sb("WP", [CC, NC, 2 * C])
        WO = [sb(f"WO{l}", [P, NG, C]) for l in range(LAYERS)]
        VB = sb("VB", [P, LAYERS, C])
        W1 = sb("W1", [CC, NC, FF])
        W2 = sb("W2", [P, FM, C])
        B1 = sb("B1", [P, FM])
        VECS = sb("VECS", [CC, 2 * len(VEC)])
        RELT = sb("RELT", [CC, 4, HPC * 32])
        RELB = sb("RELB", [CC, 3, 4, HPC * 32], BF16)
        ROPE = sb("ROPE", [CC, 2, T])
        GAVG = sb("GAVG", [CC, CC])
        ONESC = sb("ONESC", [CC, CC])
        HOT = sb("HOT", [P, T])
        MASK = sb("MASK", [P, T])
        BSEL = sb("BSEL", [P, P])
        PCOL = sb("PCOL", [P, 3])
        ABT = sb("ABT", [P, 2, NH])
        ABH = sb("ABH", [P, 2, NH], F32R)
        ABL = sb("ABL", [P, 2, NH])
        ABS = sb("ABS", [P, 3, NH])
        REGT = sb("REGT", [CC, NC, P])
        KRF = sb("KRF", [CC, NC, NREG])
        KRH = sb("KRH", [CC, NC, NREG], F32R)
        KRL = sb("KRL", [CC, NC, NREG], F32R)
        VRB = sb("VRB", [P, C])
        WARM = sb("WARM", [P, 512], BF16)
        IDF = sb("IDF", [P, P])
        IDR = sb("IDR", [P, P], F32R)
        SELM = sb("SELM", [P, GH, P], F32R)
        SELR = sb("SELR", [P, GH, 32])

        RING = [ps(f"RING{i}", [P, 2, 512]) for i in range(2)]
        PA = ps("PA", [P, 512])
        PB = ps("PB", [P, 512])
        PC = [ps(f"PC{i}", [P, 512]) for i in range(2)]

        def hidden(m):
            return PR[m // 4][:, m % 4 // 2, m % 2 * T:(m % 2 + 1) * T]

        def ring_order(l):
            r = (lambda g: [("r", l, g)]) if l == 2 else (lambda g: [])
            found = [("v", l, 0)] + ([("kr", 0, 0), ("vr", 0, 0)] if l == 0 else [])
            found += [("m", l, 0), ("m", l, 1), ("m", l, 2)] + r(0) + [("e", l, 0), ("m", l, 3), ("e", l, 1), ("m", l, 4)]
            found += r(1) + [("e", l, 2), ("m", l, 5), ("e", l, 3)] + r(2) + [("e", l, 4), ("e", l, 5)]
            if l == 1:
                found += [("f", l, m) for m in range(FM // 2)]
            return found

        def readers(kind, l, i):
            return {"v": [("v", 2)], "m": [("max", i + 1)], "e": [("probs", i + 1)], "r": [("reg probs", i + 1)],
                    "f": [("hid", 2 * i + 2)], "kr": [("kr f", NC)], "vr": [("vr", 1)]}[kind]

        uses = []
        for l in range(LAYERS):
            uses += ring_order(l)
        number = {use: n for n, use in enumerate(uses)}

        def rel_psum(w, i):
            if w == 0:
                return PC[0][0:CC, :].rearrange("p (r k c) -> p k r c", r=SIDE, k=NC)[:, i]
            return PC[1][0:CC, :].rearrange("p (c k r) -> p k r c", c=SIDE, k=NC)[:, i]

        def slot(*use):
            return RING[number[use] % 2]

        loads = [("x", X, "xT"), ("gavg", GAVG, "gavg"), ("vecs", VECS, "vecs"), ("w0", WQKV[0], "w0"),
                 ("relt", RELT, "relt"), ("vb", VB, "vb"), ("w2", WQKV[2], "w2"), ("regt", REGT, "regt")]
        loads += [("pcol", PCOL, "pcol"), ("bsel", BSEL, "bsel"), ("wo0", WO[0], "wo0"),
                 ("hot", HOT, "hot"), ("abt", ABT, "abt"), ("w1", WQKV[1], "w1"), ("wp", WP, "wp"),
                 ("rope", ROPE, "rope"), ("wo1", WO[1], "wo1"), ("ff1", W1, "ff1"), ("ff2", W2, "ff2"),
                 ("b1", B1, "b1"), ("wo2", WO[2], "wo2"), ("w3", WQKV[3], "w3"), ("wo3", WO[3], "wo3")]

        names = [f"{name} loaded" for name, _, _ in loads]
        names += ["ident", "backgrounds", "warm", "keys zero", "act chain", "dve chain", "pool chain", "hot rows",
                  "zero rows", "kr psum", "kr f", "kr parts", "kr stack", "vr psum", "vr", "ab cols",
                  "ab rows", "mask rows", "k scaled", "rel b0", "rel r", "rel b1", "rel b2", "idr", "sels",
                  "stored", "hid psum", "hid", "ff psum"]
        signals = {name: {l: count for l in range(LAYERS)} for name, count in {
            "stats": 2, "gstats": 1, "ve": 1, "y0": 1, "xn": 2, "q psum": 1, "k psum": 1, "v psum": 1, "qh": 1,
            "ql": 1, "q stack": 3 * 16, "k stack": 3 * 16, "max psum": NU, "max": NU, "v": 2, "mt psum": NG, "mt": NG,
            "scores": NU, "probs": NU, "pv": NU, "u": NG, "d psum": NG, "rd": NG, "o": NG, "y psum": 1}.items()}
        signals |= {name: {l: 1 if l == 1 else NC for l in range(LAYERS)} for name in ("qf", "kh", "kl")}
        signals |= {"kf": {1: 1}}
        signals |= {"x": {l: 3 * NC if l == 1 else NC for l in range(LAYERS)}}
        signals |= {name: {l: count for l in REL_LAYERS} for name, count in {
            "q b0": 1, "q r": 1, "q b1": 1, "q b2": 1, "q cols": 1, "rel psum": 2, "row h": NC, "col h": NC, "row l": NC,
            "col l": NC, "rel stack": 4 * 16}.items()}
        signals |= {name: {t: count for t in (1, 3)} for name, count in {
            "ln mean": 1, "dev": 2, "sq": 2, "ln var psum": 1, "ln ve": 1, "ln y0": 1, "ln t": 2, "ni": 2}.items()}
        signals |= {name: {2: NG} for name in ("reg psum", "reg probs")}
        signals |= {name: {1: 0} for name in ("kr f", "vr", "hid")}
        names += [name for name in signals if name not in names]
        sems = {name: ctx.enter_context(nc.semaphore(name.replace(" ", "_"))) for name in names}

        def sem(name):
            return sems[name]

        def upto(name, l, count):
            return sems[name], sum(c for k, c in signals[name].items() if k < l) + count

        def loaded(eng, *what):
            for name in what:
                eng.wait_ge(sem(f"{name} loaded"), 16)

        def vec(name, i):
            return VECS[:, VEC[name] + i:VEC[name] + i + 1]

        block = ctx.enter_context(nc.Block())

        @block.sync
        def _(sync):
            def load(wanted):
                for name, tile, src in wanted:
                    dst = tile[:, :, :] if len(tile.shape) == 3 else tile[:, :]
                    sync.dma_start(dst, a[src]).then_inc(sem(f"{name} loaded"), 16)

            load(loads)
            sync.wait_ge(*upto("x", 3, NC))
            sync.dma_start(out, X[:, :, :]).then_inc(sem("stored"), 16)
            sync.wait_ge(sem("stored"), 16)

        @block.gpsimd
        def _(pool):
            g = nc.gpsimd
            g.memset(WARM[:, :], 0.0).then_inc(sem("warm"), 1)
            pool.wait_ge(sem("warm"), 1)
            g.memset(IDF[:, :], 0.0).then_inc(sem("pool chain"), 1)
            pool.wait_ge(sem("pool chain"), 1)
            g.affine_select(out=IDF[:, :], in_=IDF[:, :], compare_op=ALU.not_equal, fill=1.0, base=0,
                            pattern=[[-1, P]], channel_multiplier=1).then_inc(sem("ident"), 1)
            pool.wait_ge(sem("ident"), 1)
            for col in (slice(0, KEY0), slice(REG1, KW)):
                g.memset(KS[:, :, col].bitcast(F32), 0.0).then_inc(sem("keys zero"), 1)
            pool.wait_ge(sem("keys zero"), 2)
            loaded(pool, "vecs")
            key_biases = VECS[:, 0:2 * (LAYERS + 1)]
            g.tensor_scalar(key_biases, key_biases, QK_SCALE, None, ALU.mult).then_inc(sem("k scaled"), 1)
            pool.wait_ge(sem("k scaled"), 1)

            def scale_keys(name, w):
                loaded(pool, name)
                g.tensor_scalar(w[:, :, C:2 * C], w[:, :, C:2 * C], QK_SCALE, None, ALU.mult)\
                    .then_inc(sem("k scaled"), 1)
                pool.wait_ge(sem("k scaled"), 2 + SCALED.index(name))

            scale_keys("w0", WQKV[0])
            for n, (tile, value) in enumerate((
                    (SELR[:, :, :], 0.0), (VX[:, :, :, :], 1.0), (NM[0][:, :, :].bitcast(F32), 0.0),
                    (NM[1][:, :, :].bitcast(F32), 0.0), (ONESC[:, :], 1.0 / C), (VR[:, :, :], 0.0),
                    (QS[1][96:128, :, :].bitcast(F32), 0.0))):
                g.memset(tile, value).then_inc(sem("backgrounds"), 1)
                pool.wait_ge(sem("backgrounds"), n + 1)
            pool.dma_start(KS[64:128, :, KEY0:REG1], a["hot"][64:128, None, :].to_broadcast([64, NH, T]))\
                .then_inc(sem("hot rows"), 16)
            for stack in (KS[48:64, :, KEY0:REG1], QS[0][48:64, :, :], QS[1][48:64, :, :]):
                pool.dma_start(stack, a["zeros"]).then_inc(sem("zero rows"), 16)

            def move(l, signal, src, row, done):
                pool.wait_ge(*upto(signal, l, signals[signal][l]))
                stack = KS[row:row + HD, :, KEY0:REG1] if done == "k stack" else QS[l % 2][row:row + HD, :, :]
                pool.dma_start(stack, src[:, :, :]).then_inc(sem(done), 16)

            for l in range(LAYERS):
                if l == 2:
                    pool.wait_ge(*upto("scores", 0, NU))
                    pool.dma_start(QS[0][64:128, :, :], a["mask"][64:128, None, :].to_broadcast([64, NH, T]))\
                        .then_inc(sem("mask rows"), 16)
                move(l, "qh", QH, 0, "q stack")
                move(l, "qh", QH, 16, "q stack")
                move(l, "ql", QL, 32, "q stack")
                move(l, "kh", KH, 0, "k stack")
                move(l, "kl", KL, 16, "k stack")
                move(l, "kh", KH, 32, "k stack")
                if l == 0:
                    scale_keys("w2", WQKV[2])
                if l in REL_LAYERS:
                    for w, parts in enumerate((("row h", "row l"), ("col h", "col l"))):
                        for part, src in zip(parts, (RH[w], RL[w])):
                            move(l, part, src, REL_ROWS[part], "rel stack")
                if l == 0:
                    pool.wait_ge(sem("ab cols"), 1)
                    loaded(pool, "hot")
                    for h in range(NH):
                        g.tensor_scalar(QS[1][64:96, h, :], HOT[64:96, :], ABS[64:96, 2, h:h + 1],
                                        ABS[64:96, 1, h:h + 1], ALU.mult, ALU.add).then_inc(sem("ab rows"), 1)
                        pool.wait_ge(sem("ab rows"), h + 1)
                    scale_keys("w1", WQKV[1])
                    scale_keys("wp", WP)
                    scale_keys("w3", WQKV[3])
                if l == 1:
                    pool.wait_ge(sem("kr parts"), 2)
                    for col in (0, REG1):
                        for row, src in ((0, KRH), (32, KRH), (16, KRL)):
                            pool.dma_start(KS[row:row + HD, :, col:col + NREG], src[:, :, :])\
                                .then_inc(sem("kr stack"), 16)

        @block.scalar
        def _(act):
            n = [0]

            def link(ins):
                n[0] += 1
                ins.then_inc(sem("act chain"), 1)
                act.wait_ge(sem("act chain"), n[0])

            A = nc.scalar.activation

            def rel_parts():
                loaded(act, "relt")
                A(RELB[:, 0], RELT[:, :, :], ACT.Copy).then_inc(sem("rel b0"), 1)
                act.wait_ge(sem("rel r"), 1)
                A(RELB[:, 1], RELT[:, :, :], ACT.Copy).then_inc(sem("rel b1"), 1)

            def rsqrt_gn(l):
                act.wait_ge(*upto("ve", l, 1))
                link(A(GT[:, 1, :], GT[:, 0, :], ACT.Ln))
                A(GT[:, 2, :], GT[:, 1, :], ACT.Exp, scale=-0.5).then_inc(sem("y0"), 1)

            def layer_norm(t):
                for i in range(NC):
                    act.wait_ge(*upto("dev", t, i + 1))
                    A(SQ[:, i, :], DV[:, i, :], ACT.Square).then_inc(sem("sq"), 1)
                act.wait_ge(*upto("ln ve", t, 1))
                link(A(Y0[:, :], VE[:, :], ACT.Ln))
                A(Y0[:, :], Y0[:, :], ACT.Exp, scale=-0.5).then_inc(sem("ln y0"), 1)
                g, b = ("ln1g", "ln1b") if t == 1 else ("ln3g", "ln3b")
                for i in range(NC):
                    act.wait_ge(*upto("ln t", t, i + 1))
                    A(XN[:, i, :], SQ[:, i, :], ACT.Identity, bias=vec(b, i), scale=vec(g, i))\
                        .then_inc(sem("ni"), 1)

            def queries_keys(l):
                if l != 1:
                    act.wait_ge(*upto("q psum", l, 1))
                    for i in range(NC):
                        A(QF[:, i, :], PA[0:CC, i * T:(i + 1) * T], ACT.Identity, bias=vec(f"bq{l}", i))\
                            .then_inc(sem("qf"), 1)
                if l in REL_LAYERS:
                    act.wait_ge(*upto("qf", l, NC))
                    A(QB[:, 0], QF[:, :, :], ACT.Copy).then_inc(sem("q b0"), 1)
                    act.wait_ge(*upto("q r", l, 1))
                    A(QB[:, 1], QR[:, :, :], ACT.Copy).then_inc(sem("q b1"), 1)
                if l == 1:
                    act.wait_ge(*upto("kf", l, 1))
                    A(KH[:, :, :], KF[:, :, :], ACT.Copy).then_inc(sem("kh"), 1)
                else:
                    act.wait_ge(*upto("k psum", l, 1))
                    for i in range(NC):
                        A(KH[:, i, :], PB[0:CC, i * T:(i + 1) * T], ACT.Identity, bias=vec(f"bk{l}", i))\
                            .then_inc(sem("kh"), 1)
                if l in REL_LAYERS:
                    act.wait_ge(*upto("q b2", l, 1))
                    A(QC[:, :, :, :], QB[:, :, :, :].rearrange("p t k (r c) -> p (t k) c r", r=SIDE), ACT.Copy)\
                        .then_inc(sem("q cols"), 1)
                    for w, signal in enumerate(("row h", "col h")):
                        act.wait_ge(*upto("rel psum", l, w + 1))
                        for i in range(NC):
                            A(RH[w][:, i, :].rearrange("p (r c) -> p r c", r=SIDE), rel_psum(w, i), ACT.Copy)\
                                .then_inc(sem(signal), 1)

            def maxima(l, g):
                act.wait_ge(*upto("mt psum", l, g + 1))
                if g >= 2:
                    act.wait_ge(*upto("scores", l, 2 * (g - 1)))
                A(MT[g % 2][:, :], PA[:, 0:T], ACT.Copy).then_inc(sem("mt"), 1)

            def probs(l, u):
                act.wait_ge(*upto("scores", l, u + 1))
                if u >= 3:
                    act.wait_ge(*upto("pv", l, u - 2))
                A(PR[u % 3][:, :, :], slot("e", l, u)[:, :, :], ACT.Exp).then_inc(sem("probs"), 1)

            def reg_probs(l, g):
                act.wait_ge(*upto("reg psum", l, g + 1))
                if g >= 2:
                    act.wait_ge(*upto("pv", l, 2 * (g - 1)))
                A(PG[g % 2][:, :], slot("r", l, g)[:, 0, 0:T], ACT.Exp).then_inc(sem("reg probs"), 1)

            def recip(l, g):
                act.wait_ge(*upto("d psum", l, g + 1))
                if g >= 2:
                    act.wait_ge(*upto("o", l, g - 1))
                link(A(LD[g % 2][:, :], PC[g % 2][:, T:2 * T], ACT.Ln))
                A(RD[g % 2][:, :], LD[g % 2][:, :], ACT.Exp, scale=-1.0).then_inc(sem("rd"), 1)

            act.preload_act_table_set("natural_log_exp_and_others")
            for l in range(LAYERS):
                rsqrt_gn(l)
                if l == 0:
                    rel_parts()
                if l == 1:
                    layer_norm(1)
                queries_keys(l)
                if l == 0:
                    act.wait_ge(sem("kr psum"), 1)
                    for i in range(NC):
                        A(KRF[:, i, :], slot("kr", 0, 0)[0:CC, 0, i * NREG:(i + 1) * NREG], ACT.Identity,
                          bias=vec("bk2", i)).then_inc(sem("kr f"), 1)
                maxima(l, 0)
                if l == 2:
                    reg_probs(l, 0)
                probs(l, 0)
                probs(l, 1)
                maxima(l, 1)
                if l == 2:
                    reg_probs(l, 1)
                probs(l, 2)
                recip(l, 0)
                probs(l, 3)
                maxima(l, 2)
                if l == 2:
                    reg_probs(l, 2)
                probs(l, 4)
                recip(l, 1)
                probs(l, 5)
                recip(l, 2)
                if l == 1:
                    layer_norm(3)
                    act.preload_act_table_set("gelu_and_others")
                    loaded(act, "b1")
                    for m in range(FM):
                        act.wait_ge(sem("hid psum"), m // 2 + 1)
                        A(hidden(m), slot("f", 1, m // 2)[:, m % 2, 0:T], ACT.Gelu, bias=B1[:, m:m + 1])\
                            .then_inc(sem("hid"), 1)
                    act.preload_act_table_set("natural_log_exp_and_others")

        @block.vector
        def _(dve):
            n = [0]

            def link(ins):
                n[0] += 1
                ins.then_inc(sem("dve chain"), 1)
                dve.wait_ge(sem("dve chain"), n[0])

            V = nc.vector

            def selectors():
                dve.wait_ge(sem("ident"), 1)
                V.tensor_copy(IDR[:, :], IDF[:, :]).then_inc(sem("idr"), 1)
                V.tensor_copy(SELM[:, :, :], IDF[:, 0:GH, None].to_broadcast([P, GH, P])).then_inc(sem("sels"), 1)

            def reg_selector():
                dve.wait_ge(sem("backgrounds"), 1)
                V.tensor_copy(SELR[:, :, 0:NREG], IDF[:, 0:GH, None].to_broadcast([P, GH, NREG]))\
                    .then_inc(sem("sels"), 1)

            def rel_parts():
                dve.wait_ge(sem("rel b0"), 1)
                V.tensor_tensor(RELT[:, :, :], RELT[:, :, :], RELB[:, 0], ALU.subtract).then_inc(sem("rel r"), 1)
                dve.wait_ge(sem("rel b1"), 1)
                V.tensor_tensor(RELB[:, 2], RELT[:, :, :], RELB[:, 1], ALU.subtract).then_inc(sem("rel b2"), 1)

            def bias_cols():
                loaded(dve, "abt", "pcol")
                r = slice(64, 96)
                link(V.tensor_copy(ABH[r], ABT[r]))
                link(V.tensor_tensor(ABL[r], ABT[r], ABH[r].bitcast(F32), ALU.subtract))
                link(V.tensor_scalar(ABS[r, 0:2], ABH[r].bitcast(F32), PCOL[r, 0:1], None, ALU.mult))
                link(V.scalar_tensor_tensor(out=ABS[r, 0:2], in0=ABL[r], scalar=PCOL[r, 1:2], in1=ABS[r, 0:2],
                                            op0=ALU.mult, op1=ALU.add))
                V.tensor_tensor(ABS[r, 2], ABS[r, 0], ABS[r, 1], ALU.subtract).then_inc(sem("ab cols"), 1)

            def group_norm(l, dst):
                for i in range(NC):
                    link(V.bn_stats(STAT[:, i, :], X[:, i, :]))
                for i in range(NC):
                    link(V.bn_aggr(MS[:, i, :], STAT[:, i, :]))
                for i in range(NC):
                    V.scalar_tensor_tensor(out=MS[:, i, 1:2], in0=MS[:, i, 0:1], scalar=MS[:, i, 0:1],
                                           in1=MS[:, i, 1:2], op0=ALU.mult, op1=ALU.add)\
                        .then_inc(sem("stats"), 1)
                dve.wait_ge(*upto("gstats", l, 1))
                link(V.tensor_copy(GM[:, :, :], PA[0:CC, 0:2 * NC].rearrange("p (i s) -> p i s", i=NC)))
                link(V.tensor_tensor(GT[:, 3, :], GM[:, :, 0], GM[:, :, 0], ALU.mult))
                V.scalar_tensor_tensor(out=GT[:, 0, :], in0=GM[:, :, 1], scalar=GN_EPS, in1=GT[:, 3, :],
                                       op0=ALU.add, op1=ALU.subtract).then_inc(sem("ve"), 1)
                dve.wait_ge(*upto("y0", l, 1))
                link(V.tensor_tensor(GT[:, 3, :], GT[:, 2, :], GT[:, 2, :], ALU.mult))
                link(V.scalar_tensor_tensor(out=GT[:, 4, :], in0=GT[:, 3, :], scalar=-0.5, in1=GT[:, 0, :],
                                            op0=ALU.mult, op1=ALU.mult))
                link(V.scalar_tensor_tensor(out=GT[:, 5, :], in0=GT[:, 4, :], scalar=1.5, in1=GT[:, 2, :],
                                            op0=ALU.add, op1=ALU.mult))
                for i in range(NC):
                    V.tensor_scalar(dst[:, i, :], X[:, i, :], GM[:, i, 0:1], GT[:, 5, i:i + 1],
                                    ALU.subtract, ALU.mult).then_inc(sem("xn"), 1)

            def layer_norm(t):
                dve.wait_ge(*upto("ln mean", t, 1))
                for i in range(NC):
                    V.tensor_tensor(DV[:, i, :], FL[:, i, :], PA[0:CC, 0:T], ALU.subtract)\
                        .then_inc(sem("dev"), 1)
                dve.wait_ge(*upto("ln var psum", t, 1))
                V.tensor_scalar(VE[:, :], PB[0:CC, 0:T], LN_EPS, None, ALU.add).then_inc(sem("ln ve"), 1)
                dve.wait_ge(*upto("ln y0", t, 1))
                link(V.tensor_tensor(YN[:, :], Y0[:, :], Y0[:, :], ALU.mult))
                link(V.scalar_tensor_tensor(out=YN[:, :], in0=YN[:, :], scalar=-0.5, in1=VE[:, :],
                                            op0=ALU.mult, op1=ALU.mult))
                link(V.scalar_tensor_tensor(out=YN[:, :], in0=YN[:, :], scalar=1.5, in1=Y0[:, :],
                                            op0=ALU.add, op1=ALU.mult))
                for i in range(NC):
                    V.tensor_tensor(SQ[:, i, :], DV[:, i, :], YN[:, :], ALU.mult).then_inc(sem("ln t"), 1)

            def hi_lo(src, hi, lo, src_ready, hi_signal, hi_ready, lo_signal):
                dve.wait_ge(*src_ready)
                V.tensor_copy(hi, src).then_inc(sem(hi_signal), 1)
                dve.wait_ge(*hi_ready)
                V.tensor_tensor(lo, src, hi.bitcast(F32), ALU.subtract).then_inc(sem(lo_signal), 1)

            def rotate(l, dst, plain, swapped, b, bp, ready, done):
                dve.wait_ge(*upto(ready, l, 1))
                for i in range(NC):
                    V.scalar_tensor_tensor(out=RF[0][:, i, :], in0=plain[0:CC, i * T:(i + 1) * T], scalar=vec(b, i),
                                           in1=ROPE[:, 0, :], op0=ALU.add, op1=ALU.mult)\
                        .then_inc(sem("dve chain"), 1)
                    V.scalar_tensor_tensor(out=RF[1][:, i, :], in0=swapped[0:CC, i * T:(i + 1) * T],
                                           scalar=vec(bp, i), in1=ROPE[:, 1, :], op0=ALU.add, op1=ALU.mult)\
                        .then_inc(sem("dve chain"), 1)
                n[0] += 2 * NC
                dve.wait_ge(sem("dve chain"), n[0])
                V.tensor_tensor(dst[:, :, :], RF[0][:, :, :], RF[1][:, :, :], ALU.add).then_inc(sem(done), 1)

            def queries_keys(l):
                if l == 1:
                    loaded(dve, "rope")
                    rotate(l, QF, PA, PC[0], "bq1", "bqp", "q psum", "qf")
                    hi_lo(QF[:, :, :], QH[:, :, :], QL[:, :, :], upto("qf", 1, 1), "qh", upto("qh", 1, 1), "ql")
                    rotate(l, KF, PB, PC[1], "bk1", "bkp", "k psum", "kf")
                    dve.wait_ge(*upto("kh", 1, 1))
                    V.tensor_tensor(KL[:, :, :], KF[:, :, :], KH[:, :, :].bitcast(F32), ALU.subtract)\
                        .then_inc(sem("kl"), 1)
                else:
                    if l in REL_LAYERS:
                        dve.wait_ge(*upto("q b0", l, 1))
                        V.tensor_tensor(QR[:, :, :], QF[:, :, :], QB[:, 0], ALU.subtract).then_inc(sem("q r"), 1)
                    hi_lo(QF[:, :, :], QH[:, :, :], QL[:, :, :], upto("qf", l, NC), "qh", upto("qh", l, 1), "ql")
                    if l in REL_LAYERS:
                        dve.wait_ge(*upto("q b1", l, 1))
                        V.tensor_tensor(QB[:, 2], QR[:, :, :], QB[:, 1], ALU.subtract).then_inc(sem("q b2"), 1)
                    dve.wait_ge(*upto("kh", l, NC))
                    for i in range(NC):
                        V.scalar_tensor_tensor(out=KL[:, i, :], in0=PB[0:CC, i * T:(i + 1) * T],
                                               scalar=vec(f"bk{l}", i), in1=KH[:, i, :].bitcast(F32), op0=ALU.add,
                                               op1=ALU.subtract).then_inc(sem("kl"), 1)
                dve.wait_ge(*upto("v psum", l, 1))
                if l == 0:
                    dve.wait_ge(sem("backgrounds"), 2)
                    loaded(dve, "vb")
                for c in range(2):
                    V.tensor_tensor(VX[:, c, :, 0:HD],
                                    slot("v", l, 0)[:, 0, c * C:(c + 1) * C].rearrange("p (h d) -> p h d", h=NH),
                                    VB[:, l, :].rearrange("p (h d) -> p h d", h=NH), ALU.add)\
                        .then_inc(sem("v"), 1)
                if l in REL_LAYERS:
                    for w, parts in enumerate((("row h", "row l"), ("col h", "col l"))):
                        dve.wait_ge(*upto(parts[0], l, NC))
                        for i in range(NC):
                            V.tensor_tensor(RL[w][:, i, :].rearrange("p (r c) -> p r c", r=SIDE), rel_psum(w, i),
                                            RH[w][:, i, :].bitcast(F32).rearrange("p (r c) -> p r c", r=SIDE),
                                            ALU.subtract).then_inc(sem(parts[1]), 1)

            def maximum(l, m):
                g, i = m // 2, m % 2
                if g >= 2 and i == 0:
                    dve.wait_ge(*upto("mt psum", l, g - 1))
                dve.wait_ge(*upto("max psum", l, m + 1))
                n_keys = WINDOW if l == 2 else T
                V.tensor_reduce(NM[g % 2][:, :, 2 * i:2 * i + 2].rearrange("p q j -> p j q"),
                                slot("m", l, m)[:, :, 0:2 * n_keys].rearrange("p j (q k) -> p j q k", q=2),
                                AX.X, ALU.max, negate=True).then_inc(sem("max"), 1)

            def unnormalised(l, g):
                dve.wait_ge(*upto("pv", l, 2 * g + 2))
                if g >= 2:
                    dve.wait_ge(*upto("o", l, g - 1))
                V.tensor_copy(U[g % 2][:, :], PC[g % 2][:, 0:T]).then_inc(sem("u"), 1)

            def normalised(l, g):
                dve.wait_ge(*upto("rd", l, g + 1))
                link(V.scalar_tensor_tensor(out=LD[g % 2][:, :], in0=PC[g % 2][:, T:2 * T], scalar=-1.0,
                                            in1=RD[g % 2][:, :], op0=ALU.mult, op1=ALU.mult))
                link(V.scalar_tensor_tensor(out=LD[g % 2][:, :], in0=LD[g % 2][:, :], scalar=2.0,
                                            in1=RD[g % 2][:, :], op0=ALU.add, op1=ALU.mult))
                V.tensor_tensor(O[g][:, :], LD[g % 2][:, :], U[g % 2][:, :], ALU.mult).then_inc(sem("o"), 1)

            def registers():
                hi_lo(KRF[:, :, :], KRH[:, :, :], KRL[:, :, :], (sem("kr f"), NC), "kr parts", (sem("kr parts"), 1),
                      "kr parts")
                dve.wait_ge(sem("vr psum"), 1)
                V.tensor_tensor(VRB[:, :], slot("vr", 0, 0)[:, 0, 0:C], VB[:, 2, :], ALU.add).then_inc(sem("vr"), 1)
                dve.wait_ge(sem("vr"), 1)
                dve.wait_ge(sem("backgrounds"), 7)
                loaded(dve, "pcol")
                for j in range(GH):
                    q = slice(32 * j, 32 * j + 32)
                    V.tensor_scalar(VR[q, j:NH:GH, 0:HD],
                                    VRB[q, :].rearrange("p (h d) -> p h d", h=NH)[:, j:NH:GH], PCOL[q, 2:3], None,
                                    ALU.mult).then_inc(sem("vr"), 1)
                    V.tensor_copy(VR[q, j:NH:GH, HD:32], PCOL[q, 2:3, None].to_broadcast([32, NG, HD]))\
                        .then_inc(sem("vr"), 1)

            selectors()
            loaded(dve, "x")
            for l in range(LAYERS):
                group_norm(l, FL if l == 1 else XN)
                if l == 0:
                    loaded(dve, "vecs")
                    rel_parts()
                if l == 1:
                    layer_norm(1)
                queries_keys(l)
                if l == 0:
                    registers()
                    bias_cols()
                    reg_selector()
                for m in range(5):
                    maximum(l, m)
                unnormalised(l, 0)
                maximum(l, 5)
                normalised(l, 0)
                for g in range(1, NG):
                    unnormalised(l, g)
                    normalised(l, g)
                dve.wait_ge(*upto("y psum", l, 1))
                if l != 1:
                    for i in range(NC):
                        ins = V.scalar_tensor_tensor(out=X[:, i, :], in0=PB[0:CC, i * T:(i + 1) * T],
                                                     scalar=vec(f"bo{l}", i), in1=X[:, i, :],
                                                     op0=ALU.add, op1=ALU.add)
                        ins.then_inc(sem("x"), 1)
                else:
                    for i in range(NC):
                        V.scalar_tensor_tensor(out=FL[:, i, :], in0=PB[0:CC, i * T:(i + 1) * T],
                                               scalar=vec("bo1", i), in1=FL[:, i, :],
                                               op0=ALU.add, op1=ALU.add).then_inc(sem("x"), 1)
                    dve.wait_ge(*upto("x", 1, NC))
                    layer_norm(3)
                    dve.wait_ge(sem("ff psum"), 1)
                    for i in range(NC):
                        V.scalar_tensor_tensor(out=FL[:, i, :], in0=PA[0:CC, i * T:(i + 1) * T],
                                               scalar=vec("b2", i), in1=FL[:, i, :],
                                               op0=ALU.add, op1=ALU.add).then_inc(sem("x"), 1)
                    dve.wait_ge(*upto("x", 1, 2 * NC))
                    for i in range(NC):
                        V.tensor_tensor(X[:, i, :], X[:, i, :], FL[:, i, :], ALU.add).then_inc(sem("x"), 1)
                dve.wait_ge(*upto("x", l, 3 * NC if l == 1 else NC))

        @block.tensor
        def _(pe):
            M = nc.tensor.matmul

            def take(*use):
                if number[use] >= 2:
                    former = uses[number[use] - 2]
                    for name, count in readers(*former):
                        pe.wait_ge(*upto(name, former[1], count))
                return slot(*use)

            def project(psum, w, c0, src, ready, n_ready):
                for m in range(NC):
                    for k in range(NC):
                        pe.wait_ge(ready, n_ready)
                        ins = M(psum[0:CC, m * T:(m + 1) * T], w[:, k, c0 + m * CC:c0 + (m + 1) * CC], src[:, k, :],
                                start=(k == 0), stop=(k == NC - 1))
                return ins

            def relative(l):
                pe.wait_ge(sem("rel b1"), 1)
                pe.wait_ge(sem("rel b2"), 1)
                pe.wait_ge(*upto("q b1", l, 1))
                pe.wait_ge(*upto("q b2", l, 1))
                for w in range(2):
                    if w == 1:
                        pe.wait_ge(*upto("q cols", l, 1))
                    table = 2 * REL_LAYERS.index(l) + w
                    for i in range(SIDE):
                        for t, (tp, qp) in enumerate(TERMS):
                            lhsT = RELB[:, tp, table, (SIDE - 1 - i) * HPC:(NREL - i) * HPC]
                            q = QB[:, qp, :, i * SIDE:(i + 1) * SIDE] if w == 0 else QC[:, qp * NC:(qp + 1) * NC, i, :]
                            ins = M(PC[w][0:CC, i * 2 * SIDE:(i + 1) * 2 * SIDE].rearrange("p (k c) -> p k c", k=NC),
                                    lhsT, q, start=(t == 0), stop=(t == len(TERMS) - 1))
                    ins.then_inc(sem("rel psum"), 1)

            def for_maxima(l, m):
                s = take("m", l, m)
                for k in range(2):
                    h = 2 * m + k
                    for q in range(2):
                        if l == 2:
                            keys = slice(0, WINDOW) if q == 0 else slice(REG1 + NREG - WINDOW, REG1 + NREG)
                        else:
                            keys = slice(KEY0, REG1)
                        n_keys = keys.stop - keys.start
                        ins = M(s[:, k, q * n_keys:(q + 1) * n_keys], QS[l % 2][:, h, q * P:(q + 1) * P],
                                KS[:, h, keys], start=True, stop=True)
                ins.then_inc(sem("max psum"), 1)

            def turn_maxima(l, g):
                pe.wait_ge(*upto("max", l, 2 * g + 2))
                if g == 0:
                    pe.wait_ge(sem("idr"), 1)
                    pe.wait_ge(sem("sels"), 1)
                else:
                    pe.wait_ge(*upto("mt", l, g))
                for q in range(2):
                    ins = M(PA[:, q * P:(q + 1) * P], NM[g % 2][:, q, :], IDR[:, :], start=True, stop=True)
                ins.then_inc(sem("mt psum"), 1)

            def reg_scores(l, g):
                s = take("r", l, g)
                pe.wait_ge(sem("sels"), 2)
                pe.wait_ge(*upto("mt", l, g + 1))
                for j in range(GH):
                    dst = s[32 * j:32 * j + 32, 0, 0:T]
                    M(dst, KS[:, GH * g + j, REG1:KW].bitcast(F32), QS[l % 2][:, GH * g + j, :].bitcast(F32),
                      start=True, stop=False)
                    ins = M(dst, SELR[:, j, :], MT[g % 2][:, :].bitcast(F32), start=False, stop=True)
                ins.then_inc(sem("reg psum"), 1)

            def scores(l, u):
                s = take("e", l, u)
                pe.wait_ge(*upto("mt", l, u // 2 + 1))
                for i in range(2):
                    h = 2 * u + i
                    for k in range(2):
                        dst = s[:, i, k * T:(k + 1) * T]
                        M(dst, KS[:, h, KEY0 + k * P:KEY0 + (k + 1) * P], QS[l % 2][:, h, :], start=True, stop=False)
                        ins = M(dst, SELM[:, h % GH, :], MT[u // 2 % 2][:, :], start=False, stop=True)
                ins.then_inc(sem("scores"), 1)

            def values(l, u):
                g = u // 2
                pe.wait_ge(*upto("probs", l, u + 1))
                if u == 0:
                    pe.wait_ge(*upto("v", l, 2))
                if u == 0 and l == 2:
                    pe.wait_ge(sem("vr"), 1 + 2 * GH)
                if u % 2 == 0 and g >= 2:
                    pe.wait_ge(*upto("o", l, g - 1))
                if l == 2:
                    pe.wait_ge(*upto("reg probs", l, g + 1))
                for i in range(2):
                    h = 2 * u + i
                    q = 32 * (h % GH)
                    dst = PC[g % 2][q:q + 32, 0:T]
                    for k in range(2):
                        ins = M(dst, VX[:, k, h, :], PR[u % 3][:, i, k * T:(k + 1) * T], start=(k == 0),
                                stop=(k == 1 and l != 2))
                    if l == 2:
                        ins = M(dst, VR[:, h, :], PG[g % 2][:, :], start=False, stop=True)
                ins.then_inc(sem("pv"), 1)

            def row_sums(l, g):
                if l == 0 and g == 0:
                    loaded(pe, "bsel")
                pe.wait_ge(*upto("u", l, g + 1))
                M(PC[g % 2][:, T:2 * T], BSEL[:, :], U[g % 2][:, :], start=True, stop=True)\
                    .then_inc(sem("d psum"), 1)

            def out_project(l, g):
                if g == 0:
                    loaded(pe, f"wo{l}")
                pe.wait_ge(*upto("o", l, g + 1))
                for m in range(NC):
                    ins = M(PB[0:CC, m * T:(m + 1) * T], WO[l][:, g, m * CC:(m + 1) * CC], O[g][:, :],
                            start=(g == 0 and m == 0), stop=(g == NG - 1), skip_group_check=True)
                if g == NG - 1:
                    ins.then_inc(sem("y psum"), 1)

            def registers():
                s = take("kr", 0, 0)
                loaded(pe, "w2", "regt")
                pe.wait_ge(sem("k scaled"), 2 + SCALED.index("w2"))
                for m in range(NC):
                    for k in range(NC):
                        ins = M(s[0:CC, 0, m * NREG:(m + 1) * NREG], WQKV[2][:, k, C + m * CC:C + (m + 1) * CC],
                                REGT[:, k, 0:NREG], start=(k == 0), stop=(k == NC - 1))
                ins.then_inc(sem("kr psum"), 1)
                s = take("vr", 0, 0)
                for k in range(NC):
                    ins = M(s[:, 0, 0:C], REGT[:, k, :], WQKV[2][:, k, 2 * C:3 * C], start=(k == 0),
                            stop=(k == NC - 1))
                ins.then_inc(sem("vr psum"), 1)

            def layer_norm(t, ready, n_ready):
                pe.wait_ge(ready, n_ready)
                for k in range(NC):
                    ins = M(PA[0:CC, 0:T], ONESC[:, :], FL[:, k, :], start=(k == 0), stop=(k == NC - 1))
                ins.then_inc(sem("ln mean"), 1)
                for k in range(NC):
                    pe.wait_ge(*upto("sq", t, k + 1))
                    ins = M(PB[0:CC, 0:T], ONESC[:, :], SQ[:, k, :], start=(k == 0), stop=(k == NC - 1))
                ins.then_inc(sem("ln var psum"), 1)

            def keep_warm(bank, n):
                for _ in range(n):
                    M(bank, WARM[:, 0:P], WARM[:, :], start=True, stop=True)

            pe.wait_ge(sem("warm"), 1)
            for l in range(LAYERS):
                free = take("v", l, 0)[:, 0, :]
                keep_warm(free, 9 if l == 0 else 12)
                if l == 0:
                    loaded(pe, "gavg")
                pe.wait_ge(*upto("stats", l, NC))
                M(PA[0:CC, 0:2 * NC], GAVG[:, :], MS[:, :, :], start=True, stop=True)\
                    .then_inc(sem("gstats"), 1)
                keep_warm(free, 8)
                ready = upto("xn", l, NC)
                if l == 1:
                    pe.wait_ge(sem("backgrounds"), 7)
                    layer_norm(1, *ready)
                    ready = upto("ni", 1, NC)
                loaded(pe, f"w{l}")
                last = project(PA, WQKV[l], 0, XN, *ready)
                if l == 1:
                    loaded(pe, "wp")
                    last = project(PC[0], WP, 0, XN, *ready)
                last.then_inc(sem("q psum"), 1)
                pe.wait_ge(sem("k scaled"), 2 + SCALED.index("wp" if l == 1 else f"w{l}"))
                last = project(PB, WQKV[l], C, XN, *ready)
                if l == 1:
                    last = project(PC[1], WP, C, XN, *ready)
                last.then_inc(sem("k psum"), 1)
                s = take("v", l, 0)
                for c in range(2):
                    for k in range(NC):
                        ins = M(s[:, 0, c * C:(c + 1) * C], XN[:, k, c * P:(c + 1) * P],
                                WQKV[l][:, k, 2 * C:3 * C], start=(k == 0), stop=(k == NC - 1))
                ins.then_inc(sem("v psum"), 1)
                if l in REL_LAYERS:
                    relative(l)

                if l == 0:
                    registers()
                    pe.wait_ge(sem("hot rows"), 16)
                    pe.wait_ge(sem("zero rows"), 48)
                    pe.wait_ge(sem("backgrounds"), 4)
                if l == 1:
                    pe.wait_ge(sem("ab rows"), NH)
                if l == 2:
                    pe.wait_ge(sem("mask rows"), 16)
                    pe.wait_ge(sem("kr stack"), 6 * 16)
                keep_warm(take("m", l, 0)[:, 0, :], 12 if l == 0 else 20)
                pe.wait_ge(*upto("q stack", l, 48))
                pe.wait_ge(*upto("k stack", l, 48))
                if l in REL_LAYERS:
                    pe.wait_ge(*upto("rel stack", l, 64))

                for_maxima(l, 0)
                for_maxima(l, 1)
                keep_warm(PB[:, :], 4)
                for_maxima(l, 2)
                keep_warm(PB[:, :], 3)
                turn_maxima(l, 0)
                keep_warm(PB[:, :], 2)
                if l == 2:
                    reg_scores(l, 0)
                scores(l, 0)
                for_maxima(l, 3)
                scores(l, 1)
                values(l, 0)
                for_maxima(l, 4)
                turn_maxima(l, 1)
                if l == 2:
                    reg_scores(l, 1)
                scores(l, 2)
                values(l, 1)
                for_maxima(l, 5)
                row_sums(l, 0)
                scores(l, 3)
                values(l, 2)
                turn_maxima(l, 2)
                if l == 2:
                    reg_scores(l, 2)
                scores(l, 4)
                values(l, 3)
                row_sums(l, 1)
                out_project(l, 0)
                scores(l, 5)
                values(l, 4)
                out_project(l, 1)
                values(l, 5)
                row_sums(l, 2)
                out_project(l, 2)
                if l == 1:
                    layer_norm(3, *upto("x", 1, NC))
                    loaded(pe, "ff1", "ff2")
                    pe.wait_ge(*upto("ni", 3, NC))
                    for m in range(FM // 2):
                        s = take("f", 1, m)
                        for i in range(2):
                            for k in range(NC):
                                c = 2 * m + i
                                ins = M(s[:, i, 0:T], W1[:, k, c * P:(c + 1) * P], XN[:, k, :], start=(k == 0),
                                        stop=(k == NC - 1))
                        ins.then_inc(sem("hid psum"), 1)
                    for c in range(FM):
                        pe.wait_ge(sem("hid"), c + 1)
                        for m in range(NC):
                            ins = M(PA[0:CC, m * T:(m + 1) * T], W2[:, c, m * CC:(m + 1) * CC], hidden(c),
                                    start=(c == 0 and m == 0), stop=(c == FM - 1), skip_group_check=True)
                    ins.then_inc(sem("ff psum"), 1)


def layouts(inp):
    f32 = np.float32
    heads = np.arange(NH)

    order = np.arange(C).reshape(HPC, NC, HD).transpose(1, 2, 0).reshape(C)

    def qk_order(w):
        return np.concatenate([w[..., order], w[..., C + order], w[..., 2 * C:]], -1)

    def chunks(w):
        return np.ascontiguousarray(w.reshape(NC, CC, -1).transpose(1, 0, 2))

    def column(v):
        return v.reshape(NC, CC).T

    def by_quadrant(w):
        padded = np.zeros((NG, GH, 32, C), f32)
        padded[:, :, :HD] = w.reshape(NG, GH, HD, C)
        return np.ascontiguousarray(padded.transpose(1, 2, 0, 3).reshape(P, NG, C))

    def swapped(w):
        return w.reshape(*w.shape[:-1], NH, 2, HD // 2)[..., ::-1, :].reshape(w.shape)

    def toeplitz(rel):
        t = np.zeros((HD, HPC, 32, HPC), f32)
        for r in range(HPC):
            t[:, r, :NREL, r] = rel[:NREL][::-1].T
        return t.reshape(CC, HPC * 32)

    L = {k: np.asarray(v) for k, v in inp.items()}
    wqkv = [L["L0_conv_qkv_w"], np.concatenate([L["L1_conv_wq"], L["L1_conv_wk"], L["L1_conv_wv"]], 1),
            L["L2_conv_qkv_w"].T, L["L3_conv_qkv_w"].T]
    bqkv = [L["L0_conv_qkv_b"], np.concatenate([L["L1_conv_bq"], L["L1_conv_bk"], L["L1_conv_bv"]]),
            L["L2_conv_qkv_b"], L["L3_conv_qkv_b"]]
    wqkv = [qk_order(w) for w in wqkv]
    bqkv = [qk_order(b) for b in bqkv]
    wo = [L["L0_conv_proj_w"], L["L1_conv_wo"], L["L2_conv_out_w"].T, L["L3_conv_proj_w"].T]
    bo = [L["L0_conv_proj_b"], L["L1_conv_bo"], L["L2_conv_out_b"], L["L3_conv_proj_b"]]

    vecs = np.zeros((CC, 2 * len(VEC)), f32)
    named = {f"b{v}{l}": (bqkv[l][n * C:(n + 1) * C]) for l in range(LAYERS) for n, v in enumerate("qk")}
    named |= {f"bo{l}": bo[l] for l in range(LAYERS)}
    named |= {"bqp": swapped(L["L1_conv_bq"])[order], "bkp": swapped(L["L1_conv_bk"])[order], "ln1g": L["L1_conv_ln1_g"],
              "ln1b": L["L1_conv_ln1_b"], "ln3g": L["L1_conv_ln3_g"], "ln3b": L["L1_conv_ln3_b"],
              "b2": L["L1_conv_b2"]}
    for name, v in named.items():
        vecs[:, VEC[name]:VEC[name] + NC] = column(v)

    place = np.arange(T)
    row, col, k = place // SIDE, place % SIDE, np.arange(SIDE)[:, None]
    hot = np.zeros((P, T), f32)
    hot[64:80] = hot[80:96] = row == k
    hot[96:112] = hot[112:128] = col == k
    first = np.clip(np.arange(SIDE) - 3, 0, SIDE - 7)
    mask = np.zeros((P, T), f32)
    mask[64:80] = np.where((k >= first[row]) & (k < first[row] + 7), 0, MASKED)
    mask[96:112] = np.where((k >= first[col]) & (k < first[col] + 7), 0, MASKED)
    angles = HD // 4
    timescale = np.concatenate([f32(10000.0) ** (f32(2) * np.arange(angles, dtype=f32) / f32(HD)),
                                np.full(HD // 2 - angles, np.inf, f32)]).astype(f32)
    angle = (place.astype(f32)[:, None] / timescale).astype(f32)
    sin, cos = np.sin(angle).T, np.cos(angle).T
    rope = np.stack([np.repeat(np.concatenate([cos, cos]), HPC, 0), np.repeat(np.concatenate([-sin, sin]), HPC, 0)], 1)
    group = np.arange(CC) // GN_GROUP
    pcol = np.zeros((P, 3), f32)
    pcol[64:80, 0] = 1
    pcol[80:96, 1] = 1
    pcol[:, 2] = np.arange(P) % 32 < NREG
    bsel = np.zeros((P, P), f32)
    for j in range(GH):
        bsel[32 * j + HD, 32 * j:32 * j + 32] = 1
    abt = np.zeros((P, 2, NH), f32)
    abt[64:96] = L["L1_conv_attn_biases"].T
    regt = np.zeros((CC, NC, GH, 32), f32)
    regt[:, :, :, :NREG] = chunks(L["L2_conv_registers"].T)[:, :, None, :]

    arrays = {"xT": chunks(L["x"].reshape(T, C).T), "vecs": vecs, "gavg": (group[:, None] == group) / f32(GN_GROUP),
              "pcol": pcol, "relt": np.stack([toeplitz(L[f"L{l}_conv_rel_pos_{v}"]) for l in REL_LAYERS for v in "hw"], 1),
              "hot": hot, "zeros": np.zeros((HD, NH, T), f32), "mask": mask, "abt": abt, "bsel": bsel, "rope": rope, "regt": regt.reshape(CC, NC, P),
              "vb": np.broadcast_to(np.stack([b[2 * C:] for b in bqkv]), (P, LAYERS, C)),
              "wp": chunks(np.concatenate([swapped(L["L1_conv_wq"])[:, order], swapped(L["L1_conv_wk"])[:, order]], 1)),
              "ff1": chunks(L["L1_conv_w1"]), "ff2": L["L1_conv_w2"].reshape(FM, P, C).transpose(1, 0, 2),
              "b1": L["L1_conv_b1"].reshape(FM, P).T}
    for l in range(LAYERS):
        arrays[f"w{l}"] = chunks(wqkv[l])
        arrays[f"wo{l}"] = by_quadrant(wo[l])
    return {name: np.ascontiguousarray(v, dtype=f32) for name, v in arrays.items()}


def kernel(**inputs):
    import concourse.bacc as bacc
    from concourse.bass_utils import run_bass_kernel_spmd

    nc = bacc.Bacc("TRN2", target_bir_lowering=False, num_devices=1)
    arrays = layouts(inputs)
    args = {name: nc.dram_tensor(f"in_{name}", v.shape, F32, kind="ExternalInput").ap() for name, v in arrays.items()}
    out = nc.dram_tensor("out_xT", (CC, NC, T), F32, kind="ExternalOutput").ap()
    build(nc, args, out)
    r = run_bass_kernel_spmd(nc, [{f"in_{name}": v for name, v in arrays.items()}], core_ids=[0])
    got = r.results[0]["out_xT"]
    return got.transpose(2, 1, 0).reshape(1, SIDE, SIDE, C)
```

```python
from contextlib import ExitStack

import numpy as np

import concourse.bass as bass
from concourse import mybir
from concourse.alu_op_type import AluOpType as ALU

ACT = mybir.ActivationFunctionType
AX = mybir.AxisListType
F32 = mybir.dt.float32
F32R = mybir.dt.float32r
BF16 = mybir.dt.bfloat16

SIDE = 16
T = SIDE * SIDE
C = 192
CC = 96
NC = C // CC
HD = 16
NH = C // HD
HPC = CC // HD
P = 128
NG = 3
GH = 4
NPR = 6
DMA_WARM = (3, 22, 17, 21)
AHEAD = 7
EARLY = 2
NREG = 16
FF = 768
FM = FF // P
KEY0 = NREG
REG1 = KEY0 + T
KW = REG1 + 32
WINDOW = NREG + (SIDE // 2 + 3) * SIDE
GN_GROUP = C // 32
GN_EPS = 1e-5
LN_EPS = 1e-5
NREL = 2 * SIDE - 1
QK_SCALE = HD ** -0.5
MASKED = -2.0 ** 100
LAYERS = 4
REL_LAYERS = (0, 3)
TERMS = ((0, 0), (0, 1), (1, 2))
Q2 = NG * P

VEC = {name: 2 * n for n, name in enumerate(
    [f"bk{l}" for l in range(LAYERS)] + ["bkp"]
    + [f"{v}{l}" for l in range(LAYERS) for v in ("bq", "bo")] + ["bqp", "ln1g", "ln1b", "ln3g", "ln3b", "b2"])}

SCALED = ("w0", "w2", "w1", "wp", "w3")



def build(nc, a, out):
    with ExitStack() as ctx:
        def sb(name, shape, dt=F32):
            return ctx.enter_context(nc.sbuf_tensor(name, shape, dt))

        def key_column(l):
            return Q2 if l in REL_LAYERS else C

        def ps(name, shape):
            return ctx.enter_context(nc.psum_tensor(name, shape, F32))

        X = sb("X", [CC, NC, T])
        XN = sb("XN", [CC, NC, T])
        FL = sb("FL", [CC, NC, T])
        DV = sb("DV", [CC, NC, T])
        SQ = sb("SQ", [CC, NC, T])
        EPS = sb("EPS", [P, 1])
        VE = sb("VE", [CC, T])
        Y0 = sb("Y0", [CC, T])
        YN = sb("YN", [CC, T])
        QF = sb("QF", [CC, NC, T])
        KF = sb("KF", [CC, NC, T])
        QH = sb("QH", [CC, NC, T], F32R)
        QL = sb("QL", [CC, NC, T], F32R)
        KH = sb("KH", [CC, NC, T], F32R)
        KL = sb("KL", [CC, NC, T], F32R)
        QD = sb("QD", [P, NG, T])
        QHL = sb("QHL", [P, NG, T], F32R)
        QB = sb("QB", [P, 2, NG, T], BF16)
        QC = sb("QC", [P, 2 * NG, SIDE, SIDE], BF16)
        QR = sb("QR", [P, NG, T])
        Q1 = sb("Q1", [64, NG, T], BF16)
        RF = [sb(f"RF{i}", [CC, NC, T]) for i in range(2)]
        RH = sb("RH", [P, NG, T], F32R)
        RL = sb("RL", [P, NG, T], F32R)
        QS = [sb(f"QS{i}", [P, NH, T], F32R) for i in range(2)]
        KS = sb("KS", [P, NH, KW], F32R)
        VX = sb("VX", [P, 2, NH, 32])
        VR = sb("VR", [P, NH, 32])
        PR = sb("PR", [P, NPR, 2 * T])
        PG = [sb(f"PG{i}", [P, T]) for i in range(2)]
        NM = [sb(f"NM{i}", [P, 2, P], F32R) for i in range(2)]
        MT = [sb(f"MT{i}", [P, T], F32R) for i in range(2)]
        U = [sb(f"U{i}", [P, T]) for i in range(2)]
        LD = [sb(f"LD{i}", [P, T]) for i in range(2)]
        RD = [sb(f"RD{i}", [P, T]) for i in range(2)]
        O = [sb(f"O{i}", [P, T]) for i in range(NG)]
        STAT = sb("STAT", [CC, NC, 6])
        MS = sb("MS", [CC, NC, 2])
        GM = sb("GM", [CC, NC, 2])
        GT = sb("GT", [CC, 6, NC])

        WQKV = [sb(f"WQKV{l}", [CC, NC, key_column(l) + 2 * C]) for l in range(LAYERS)]
        WP = sb("WP", [CC, NC, 2 * C])
        WO = [sb(f"WO{l}", [P, NG, C]) for l in range(LAYERS)]
        VB = sb("VB", [P, LAYERS, C])
        W1 = sb("W1", [CC, NC, FF])
        W2 = sb("W2", [P, FM, C])
        B1 = sb("B1", [P, FM])
        VECS = sb("VECS", [CC, 2 * len(VEC)])
        QBIAS = sb("QBIAS", [P, len(REL_LAYERS), NG])
        RELT = sb("RELT", [P, 4, GH * 32])
        RELB = sb("RELB", [P, 3, 4, GH * 32], BF16)
        ROPE = sb("ROPE", [CC, 2, T])
        GAVG = sb("GAVG", [CC, CC])
        ONESC = sb("ONESC", [CC, CC])
        HOT = sb("HOT", [P, T])
        BSEL = sb("BSEL", [P, P])
        PCOL = sb("PCOL", [P, 3])
        ABT = sb("ABT", [P, 2, NH])
        ABH = sb("ABH", [P, 2, NH], F32R)
        ABL = sb("ABL", [P, 2, NH])
        ABS = sb("ABS", [P, 3, NH])
        REGT = sb("REGT", [CC, NC, P])
        KRF = sb("KRF", [CC, NC, NREG])
        KRH = sb("KRH", [CC, NC, NREG], F32R)
        KRL = sb("KRL", [CC, NC, NREG], F32R)
        VRB = sb("VRB", [P, C])
        WARM = sb("WARM", [P, 512], BF16)
        IDF = sb("IDF", [P, P])
        IDR = sb("IDR", [P, P], F32R)
        SELM = sb("SELM", [P, GH, P], F32R)
        SELR = sb("SELR", [P, GH, 32])

        RINGS = [[ps(f"RING{r}{i}", [P, 512]) for i in range(2)] for r in range(2)]
        PA = ps("PA", [P, 512])
        PB = ps("PB", [P, 512])
        PC = [ps(f"PC{i}", [P, 512]) for i in range(2)]

        def hidden(m):
            return PR[:, m // 2, m % 2 * T:(m % 2 + 1) * T]

        RING_OF = {"v": 0, "kr": 0, "vr": 0, "m": 0, "q": 1, "r": 1, "e": 1, "f": 1}

        def ring_order(l):
            found = [("v", l, 0)] + ([("kr", 0, 0), ("vr", 0, 0)] if l == 0 else [])
            found += [("m", l, h) for h in range(NH)]
            found += [("q", l, 0)] if l in REL_LAYERS else []
            for h in range(NH):
                if l == 2 and h in (EARLY, GH, 2 * GH):
                    found.append(("r", l, h // GH))
                found.append(("e", l, h))
            if l == 1:
                found += [("f", l, m) for m in range(FM // 2)]
            return found

        def readers(kind, l, i):
            return {"v": [("v", 2)], "m": [("max", i + 1)], "e": [("probs", i + 1)], "r": [("reg probs", i + 1)],
                    "f": [("hid", 2 * i + 2)], "kr": [("kr f", NC)], "q": [("qf", NG)], "vr": [("vr", 1)]}[kind]

        uses = [[], []]
        for l in range(LAYERS):
            for use in ring_order(l):
                uses[RING_OF[use[0]]].append(use)
        number = {use: n for ring in uses for n, use in enumerate(ring)}

        def rel_psum(w, b):
            if w == 0:
                return PC[b][0:64, 0:NG * P].rearrange("p (r g c) -> p g r c", r=SIDE // 2, g=NG)
            return PC[b][64:128, 0:NG * P].rearrange("p (c g r) -> p g r c", c=SIDE // 2, g=NG)

        def q_psum(l, g):
            return PA[:, g * T:(g + 1) * T] if g < 2 else slot("q", l, 0)[:, 0:T]

        def chunk_psum(part, l, i):
            bank = PA if part == "q" else PB
            if l == 2 and i:
                return PC[part == "k"][0:CC, 0:T]
            return bank[0:CC, i * T:(i + 1) * T]

        def rel_part(tile, w, b):
            if w == 0:
                return tile[0:64, :, :].rearrange("p g (b r c) -> p b g r c", b=2, r=SIDE // 2)[:, b]
            return tile[64:128, :, :].rearrange("p g (r b c) -> p b g r c", r=SIDE, b=2)[:, b]

        def slot(*use):
            return RINGS[RING_OF[use[0]]][number[use] % 2]

        loads = [("x", X, "xT"), ("gavg", GAVG, "gavg"), ("vecs", VECS, "vecs"), ("w0", WQKV[0], "w0"),
                 ("qbias", QBIAS, "qbias"), ("relt", RELT, "relt"), ("vb", VB, "vb"), ("w2", WQKV[2], "w2"), ("regt", REGT, "regt")]
        loads += [("pcol", PCOL, "pcol"), ("bsel", BSEL, "bsel"), ("wo0", WO[0], "wo0"),
                 ("hot", HOT, "hot"), ("abt", ABT, "abt")]
        later_loads = [
                 ("w1", WQKV[1], "w1"), ("wp", WP, "wp"),
                 ("rope", ROPE, "rope"), ("wo1", WO[1], "wo1"), ("ff1", W1, "ff1"), ("ff2", W2, "ff2"),
                 ("b1", B1, "b1"), ("wo2", WO[2], "wo2"), ("w3", WQKV[3], "w3"), ("wo3", WO[3], "wo3")]

        names = [f"{name} loaded" for name, _, _ in loads + later_loads]
        names += ["ident", "backgrounds", "warm", "keys zero", "act chain", "dve chain", "pool chain", "hot rows",
                  "zero rows", "kr psum", "kr f", "kr parts", "kr stack", "vr psum", "vr", "ab cols",
                  "ab rows", "mask rows", "k scaled", "rel b0", "rel r", "rel b1", "rel b2", "idr", "sels",
                  "stored", "hid psum", "hid", "ff psum"]
        signals = {name: {l: count for l in range(LAYERS)} for name, count in {
            "channel stats": NC, "channel means": NC, "stats": 2, "gstats": 1, "ve": 1, "gm": 1, "y0": 1, "xn": 2,
            "v psum": 1, "k stack": 3 * 16, "max psum": NH, "max": NH, "v": 2, "early psum": 1, "early": 1, "mt psum": NG, "mt": NG,
            "scores": NH, "probs": NH, "pv": NH, "u": NG, "d psum": NG, "rd": NG, "o": NG, "y psum": 1}.items()}
        signals |= {name: {l: 1 if l == 1 else NC for l in range(LAYERS)} for name in ("kh", "kl")}
        signals |= {"q psum": {0: NG, 1: 1, 2: NC, 3: NG}, "k psum": {0: 1, 1: 1, 2: NC, 3: 1},
                    "q plain": {1: 1}, "k plain": {1: 1}, "qf": {0: NG, 1: 1, 2: 0, 3: NG},
                    "qh": {0: NG, 1: 1, 2: NC, 3: NG}, "ql": {0: 1, 1: 1, 2: NC, 3: 1},
                    "q stack": {0: 2 * 16, 1: 3 * 16, 2: 3 * 16, 3: 2 * 16}}
        signals |= {"kf": {1: 1}}
        signals |= {"x": {l: 3 * NC if l == 1 else NC for l in range(LAYERS)}}
        signals |= {name: {l: count for l in REL_LAYERS} for name, count in {
            "q b0": NG, "q b0 copy": 1, "q r": 1, "q b1": 1, "q1": 1, "q b2": 1, "q cols": 2, "rel psum": 4, "rel h": 4, "rel l": 4,
            "rel stack": 4 * 16}.items()}
        signals |= {name: {t: count for t in (1, 3)} for name, count in {
            "ln mean": 1, "dev": 2, "sq": 2, "ln var psum": 1, "ln ve": 1, "ln ln": 1, "ln y0": 1, "ln t": 2, "ni": 2}.items()}
        signals |= {name: {2: NG} for name in ("reg psum", "reg probs")}
        signals |= {name: {1: 0} for name in ("kr f", "vr", "hid")}
        names += [name for name in signals if name not in names]
        sems = {name: ctx.enter_context(nc.semaphore(name.replace(" ", "_"))) for name in names}

        def sem(name):
            return sems[name]

        def upto(name, l, count):
            return sems[name], sum(c for k, c in signals[name].items() if k < l) + count

        def loaded(eng, *what):
            for name in what:
                eng.wait_ge(sem(f"{name} loaded"), 16)

        def vec(name, i):
            return VECS[:, VEC[name] + i:VEC[name] + i + 1]

        block = ctx.enter_context(nc.Block())

        @block.sync
        def _(sync):
            def load(wanted):
                for name, tile, src in wanted:
                    dst = tile[:, :, :] if len(tile.shape) == 3 else tile[:, :]
                    sync.dma_start(dst, a[src]).then_inc(sem(f"{name} loaded"), 16)

            load(loads)
            for l in range(LAYERS):
                def move(signal, stack, src, done, count=None):
                    sync.wait_ge(*upto(signal, l, count or signals[signal][l]))
                    sync.dma_start(stack.bitcast(F32), src.bitcast(F32)).then_inc(sem(done), 16)

                queries = QS[l % 2]
                if l in REL_LAYERS:
                    move("qh", queries[32:48, :, :], QHL[0:64, :, :], "q stack")
                else:
                    for row in (0, 32):
                        move("qh", queries[row:row + HD, :, :], QH[:, :, :], "q stack")
                    move("ql", queries[16:32, :, :], QL[:, :, :], "q stack")
                for row in (0, 16):
                    move("kh", KS[row:row + HD, :, KEY0:REG1], KH[:, :, :], "k stack")
                if l in REL_LAYERS:
                    move("ql", queries[0:32, :, :], QHL[:, :, :], "q stack")
                move("kl", KS[32:48, :, KEY0:REG1], KL[:, :, :], "k stack")
                if l in REL_LAYERS:
                    for w in range(2):
                        for name, row, src in (("rel h", 64, RH), ("rel l", 96, RL)):
                            move(name, queries[row + HD * w:row + HD * w + HD, :, :], src[64 * w:64 * w + 64, :, :],
                                 "rel stack", 2 * w + 2)
                if l == 0:
                    sync.wait_ge(*upto("rel stack", 0, 64))
                    load(later_loads)
            sync.wait_ge(*upto("x", 3, NC))
            sync.dma_start(out, X[:, :, :]).then_inc(sem("stored"), 16)
            sync.wait_ge(sem("stored"), 16)

        @block.gpsimd
        def _(pool):
            g = nc.gpsimd
            g.memset(WARM[:, :], 0.0).then_inc(sem("warm"), 1)
            pool.wait_ge(sem("warm"), 1)
            g.memset(IDF[:, :], 0.0).then_inc(sem("pool chain"), 1)
            pool.wait_ge(sem("pool chain"), 1)
            g.affine_select(out=IDF[:, :], in_=IDF[:, :], compare_op=ALU.not_equal, fill=1.0, base=0,
                            pattern=[[-1, P]], channel_multiplier=1).then_inc(sem("ident"), 1)
            pool.wait_ge(sem("ident"), 1)
            for col in (slice(0, KEY0), slice(REG1, KW)):
                g.memset(KS[:, :, col].bitcast(F32), 0.0).then_inc(sem("keys zero"), 1)
            pool.wait_ge(sem("keys zero"), 2)
            pool.dma_start(KS[64:128, :, KEY0:REG1], a["hot"][64:128, None, :].to_broadcast([64, NH, T]))\
                .then_inc(sem("hot rows"), 16)
            for stack in (KS[48:64, :, KEY0:REG1], QS[0][48:64, :, :], QS[1][48:64, :, :]):
                pool.dma_start(stack, a["zeros"]).then_inc(sem("zero rows"), 16)

            loaded(pool, "vecs")
            key_biases = VECS[:, 0:2 * (LAYERS + 1)]
            g.tensor_scalar(key_biases, key_biases, QK_SCALE, None, ALU.mult).then_inc(sem("k scaled"), 1)
            pool.wait_ge(sem("k scaled"), 1)

            def scale_keys(name, w, first=C):
                loaded(pool, name)
                g.tensor_scalar(w[:, :, first:first + C], w[:, :, first:first + C], QK_SCALE, None, ALU.mult)\
                    .then_inc(sem("k scaled"), 1)
                pool.wait_ge(sem("k scaled"), 2 + SCALED.index(name))

            scale_keys("w0", WQKV[0], Q2)
            for n, (tile, value) in enumerate((
                    (SELR[:, :, :], 0.0), (VX[:, :, :, :], 1.0), (NM[0][:, :, :].bitcast(F32), 0.0),
                    (NM[1][:, :, :].bitcast(F32), 0.0), (ONESC[:, :], 1.0 / C), (EPS[:, :], LN_EPS), (VR[:, :, :], 0.0))):
                g.memset(tile, value).then_inc(sem("backgrounds"), 1)
                pool.wait_ge(sem("backgrounds"), n + 1)
            scale_keys("w2", WQKV[2])

            for l in range(LAYERS):
                if l == 2:
                    pool.wait_ge(*upto("scores", 0, NH))
                    pool.dma_start(QS[0][64:128, :, :], a["mask"][64:128, None, :].to_broadcast([64, NH, T]))\
                        .then_inc(sem("mask rows"), 16)
                if l == 0:
                    pool.wait_ge(sem("ab cols"), 1)
                    loaded(pool, "hot")
                    for h in range(NH):
                        g.tensor_scalar(QS[1][64:128, h, :], HOT[64:128, :], ABS[64:128, 2, h:h + 1],
                                        ABS[64:128, 1, h:h + 1], ALU.mult, ALU.add).then_inc(sem("ab rows"), 1)
                        pool.wait_ge(sem("ab rows"), h + 1)
                    scale_keys("w1", WQKV[1])
                    scale_keys("wp", WP)
                    scale_keys("w3", WQKV[3], Q2)
                if l == 1:
                    pool.wait_ge(sem("kr parts"), 2)
                    for col in (0, REG1):
                        for row, src in ((0, KRH), (16, KRH), (32, KRL)):
                            pool.dma_start(KS[row:row + HD, :, col:col + NREG], src[:, :, :])\
                                .then_inc(sem("kr stack"), 16)

        @block.scalar
        def _(act):
            n = [0]

            def link(ins):
                n[0] += 1
                ins.then_inc(sem("act chain"), 1)
                act.wait_ge(sem("act chain"), n[0])

            A = nc.scalar.activation

            def rel_parts():
                loaded(act, "relt")
                A(RELB[:, 0], RELT[:, :, :], ACT.Copy).then_inc(sem("rel b0"), 1)
                A(RELB[0:64, 2], RELT[0:64, :, :], ACT.Copy).then_inc(sem("rel b0"), 1)
                act.wait_ge(sem("rel r"), 1)
                A(RELB[:, 1], RELT[:, :, :], ACT.Copy).then_inc(sem("rel b1"), 1)

            def rsqrt_gn(l):
                act.wait_ge(*upto("ve", l, 1))
                link(A(GT[:, 1, :], GT[:, 0, :], ACT.Ln))
                A(GT[:, 2, :], GT[:, 1, :], ACT.Exp, scale=-0.5).then_inc(sem("y0"), 1)

            def layer_norm(t):
                for i in range(NC):
                    act.wait_ge(*upto("dev", t, i + 1))
                    A(SQ[:, i, :], DV[:, i, :], ACT.Square).then_inc(sem("sq"), 1)
                act.wait_ge(*upto("ln var psum", t, 1))
                A(Y0[:, :], PB[0:CC, 0:T], ACT.Ln, bias=EPS[0:CC, :]).then_inc(sem("ln ln"), 1)
                act.wait_ge(*upto("ln ln", t, 1))
                A(Y0[:, :], Y0[:, :], ACT.Exp, scale=-0.5).then_inc(sem("ln y0"), 1)
                g, b = ("ln1g", "ln1b") if t == 1 else ("ln3g", "ln3b")
                for i in range(NC):
                    act.wait_ge(*upto("ln t", t, i + 1))
                    A(XN[:, i, :], SQ[:, i, :], ACT.Identity, bias=vec(b, i), scale=vec(g, i))\
                        .then_inc(sem("ni"), 1)

            def k_high(l):
                for i in range(NC):
                    act.wait_ge(*upto("k psum", l, i + 1 if l == 2 else 1))
                    A(KH[:, i, :], chunk_psum("k", l, i), ACT.Identity, bias=vec(f"bk{l}", i)).then_inc(sem("kh"), 1)

            def queries_keys(l):
                if l == 1:
                    act.wait_ge(*upto("qf", 1, 1))
                    A(QH[:, :, :], QF[:, :, :], ACT.Copy).then_inc(sem("qh"), 1)
                if l == 2:
                    for i in range(NC):
                        act.wait_ge(*upto("q psum", l, i + 1))
                        A(QH[:, i, :], chunk_psum("q", l, i), ACT.Identity, bias=vec("bq2", i))\
                            .then_inc(sem("qh"), 1)
                if l in REL_LAYERS:
                    if l == 0:
                        loaded(act, "qbias")
                    for g in range(NG):
                        act.wait_ge(*upto("q psum", l, max(g + 1, 2)))
                        A(QD[:, g, :], q_psum(l, g), ACT.Identity, bias=QBIAS[:, REL_LAYERS.index(l), g:g + 1])\
                            .then_inc(sem("qf"), 1)
                    act.wait_ge(*upto("qf", l, NG))
                    A(QB[64:128, 1], QD[64:128, :, :], ACT.Copy).then_inc(sem("q b0 copy"), 1)
                if l == 2:
                    k_high(l)
                if l in REL_LAYERS:
                    act.wait_ge(*upto("q r", l, 1))
                    A(QB[64:128, 0], QR[64:128, :, :], ACT.Copy).then_inc(sem("q b1"), 1)
                    k_high(l)
                    act.wait_ge(*upto("q b1", l, 1))
                    A(cols(0), rows(0), ACT.Copy).then_inc(sem("q cols"), 1)
                    act.wait_ge(*upto("q b2", l, 1))
                    A(cols(1), rows(1), ACT.Copy).then_inc(sem("q cols"), 1)
                    for w in range(2):
                        for b in range(2):
                            act.wait_ge(*upto("rel psum", l, 2 * w + b + 1))
                            A(rel_part(RH, w, b), rel_psum(w, b), ACT.Copy).then_inc(sem("rel h"), 1)

            def cols(pair):
                return QC[:, pair * NG:(pair + 1) * NG, :, :]

            def rows(pair):
                return QB[:, pair].rearrange("p g (r c) -> p g c r", r=SIDE)

            def early_maxima(l):
                act.wait_ge(*upto("early psum", l, 1))
                A(MT[1][0:EARLY, :], PA[0:EARLY, 0:T], ACT.Copy).then_inc(sem("early"), 1)

            def maxima(l, g):
                act.wait_ge(*upto("mt psum", l, g + 1))
                if g:
                    act.wait_ge(*upto("scores", l, GH * (g - 1) if g > 1 else EARLY))
                A(MT[g % 2][:, :], PA[:, 0:T], ACT.Copy).then_inc(sem("mt"), 1)

            def probs(l, h):
                act.wait_ge(*upto("scores", l, h + 1))
                if h >= NPR:
                    act.wait_ge(*upto("pv", l, h - NPR + 1))
                A(PR[:, h % NPR, :], slot("e", l, h)[:, :], ACT.Exp).then_inc(sem("probs"), 1)

            def reg_probs(l, g):
                act.wait_ge(*upto("reg psum", l, g + 1))
                if g >= 2:
                    act.wait_ge(*upto("pv", l, GH * (g - 1)))
                A(PG[g % 2][:, :], slot("r", l, g)[:, 0:T], ACT.Exp).then_inc(sem("reg probs"), 1)

            def recip(l, g):
                act.wait_ge(*upto("d psum", l, g + 1))
                if g >= 2:
                    act.wait_ge(*upto("o", l, g - 1))
                link(A(LD[g % 2][:, :], PC[g % 2][:, T:2 * T], ACT.Ln))
                A(RD[g % 2][:, :], LD[g % 2][:, :], ACT.Exp, scale=-1.0).then_inc(sem("rd"), 1)

            act.preload_act_table_set("natural_log_exp_and_others")
            for l in range(LAYERS):
                rsqrt_gn(l)
                if l == 0:
                    rel_parts()
                if l == 1:
                    act.wait_ge(sem("backgrounds"), 7)
                    layer_norm(1)
                queries_keys(l)
                if l == 0:
                    act.wait_ge(sem("kr psum"), 1)
                    for i in range(NC):
                        A(KRF[:, i, :], slot("kr", 0, 0)[0:CC, i * NREG:(i + 1) * NREG], ACT.Identity,
                          bias=vec("bk2", i)).then_inc(sem("kr f"), 1)
                early_maxima(l)
                for h in range(NH):
                    if l == 2 and h in (EARLY, GH, 2 * GH):
                        reg_probs(l, h // GH)
                    if h in (1, GH - 1):
                        maxima(l, h // 2)
                    probs(l, h)
                    if h == GH + 2:
                        maxima(l, 2)
                    if h == GH + 2:
                        recip(l, 0)
                    if h == 2 * GH + 2:
                        recip(l, 1)
                recip(l, 2)
                if l == 1:
                    layer_norm(3)
                    act.preload_act_table_set("gelu_and_others")
                    loaded(act, "b1")
                    for m in range(FM):
                        act.wait_ge(sem("hid psum"), m // 2 + 1)
                        A(hidden(m), slot("f", 1, m // 2)[:, m % 2 * T:(m % 2 + 1) * T], ACT.Gelu, bias=B1[:, m:m + 1])\
                            .then_inc(sem("hid"), 1)
                    act.preload_act_table_set("natural_log_exp_and_others")

        @block.vector
        def _(dve):
            n = [0]

            def link(ins):
                n[0] += 1
                ins.then_inc(sem("dve chain"), 1)
                dve.wait_ge(sem("dve chain"), n[0])

            V = nc.vector

            def selectors():
                dve.wait_ge(sem("ident"), 1)
                V.tensor_copy(IDR[:, :], IDF[:, :]).then_inc(sem("idr"), 1)
                V.tensor_copy(SELM[:, :, :], IDF[:, 0:GH, None].to_broadcast([P, GH, P])).then_inc(sem("sels"), 1)

            def reg_selector():
                dve.wait_ge(sem("backgrounds"), 1)
                V.tensor_copy(SELR[:, :, 0:NREG], IDF[:, 0:GH, None].to_broadcast([P, GH, NREG]))\
                    .then_inc(sem("sels"), 1)

            def rel_parts():
                dve.wait_ge(sem("rel b0"), 2)
                V.tensor_tensor(RELT[:, :, :], RELT[:, :, :], RELB[:, 0], ALU.subtract).then_inc(sem("rel r"), 1)
                dve.wait_ge(sem("rel b1"), 1)
                V.tensor_tensor(RELB[64:128, 2], RELT[64:128, :, :], RELB[64:128, 1], ALU.subtract)\
                    .then_inc(sem("rel b2"), 1)

            def bias_cols():
                loaded(dve, "abt", "pcol")
                r = slice(64, 128)
                link(V.tensor_copy(ABH[r], ABT[r]))
                link(V.tensor_tensor(ABL[r], ABT[r], ABH[r].bitcast(F32), ALU.subtract))
                link(V.tensor_scalar(ABS[r, 0:2], ABH[r].bitcast(F32), PCOL[r, 0:1], None, ALU.mult))
                link(V.scalar_tensor_tensor(out=ABS[r, 0:2], in0=ABL[r], scalar=PCOL[r, 1:2], in1=ABS[r, 0:2],
                                            op0=ALU.mult, op1=ALU.add))
                V.tensor_tensor(ABS[r, 2], ABS[r, 0], ABS[r, 1], ALU.subtract).then_inc(sem("ab cols"), 1)

            def group_norm(l, dst):
                for i in range(NC):
                    if l:
                        dve.wait_ge(*upto("x", l - 1, signals["x"][l - 1] - NC + i + 1))
                    V.bn_stats(STAT[:, i, :], X[:, i, :]).then_inc(sem("channel stats"), 1)
                for i in range(NC):
                    dve.wait_ge(*upto("channel stats", l, i + 1))
                    V.bn_aggr(MS[:, i, :], STAT[:, i, :]).then_inc(sem("channel means"), 1)
                for i in range(NC):
                    dve.wait_ge(*upto("channel means", l, i + 1))
                    V.scalar_tensor_tensor(out=MS[:, i, 1:2], in0=MS[:, i, 0:1], scalar=MS[:, i, 0:1],
                                           in1=MS[:, i, 1:2], op0=ALU.mult, op1=ALU.add)\
                        .then_inc(sem("stats"), 1)
                dve.wait_ge(*upto("gstats", l, 1))
                group = PA[0:CC, 0:2 * NC].rearrange("p (i s) -> p i s", i=NC)
                for i in range(NC):
                    n[0] += 1
                    V.tensor_scalar(GT[:, 3, i:i + 1], group[:, i, 0:1], group[:, i, 0:1], None, ALU.mult)\
                        .then_inc(sem("dve chain"), 1)
                dve.wait_ge(sem("dve chain"), n[0])
                V.scalar_tensor_tensor(out=GT[:, 0, :], in0=group[:, :, 1], scalar=GN_EPS, in1=GT[:, 3, :],
                                       op0=ALU.add, op1=ALU.subtract).then_inc(sem("ve"), 1)
                V.tensor_copy(GM[:, :, :], group).then_inc(sem("gm"), 1)
                dve.wait_ge(*upto("y0", l, 1))
                link(V.tensor_tensor(GT[:, 3, :], GT[:, 2, :], GT[:, 2, :], ALU.mult))
                link(V.scalar_tensor_tensor(out=GT[:, 4, :], in0=GT[:, 3, :], scalar=-0.5, in1=GT[:, 0, :],
                                            op0=ALU.mult, op1=ALU.mult))
                link(V.scalar_tensor_tensor(out=GT[:, 5, :], in0=GT[:, 4, :], scalar=1.5, in1=GT[:, 2, :],
                                            op0=ALU.add, op1=ALU.mult))
                dve.wait_ge(*upto("gm", l, 1))
                for i in range(NC):
                    V.tensor_scalar(dst[:, i, :], X[:, i, :], GM[:, i, 0:1], GT[:, 5, i:i + 1],
                                    ALU.subtract, ALU.mult).then_inc(sem("xn"), 1)

            def layer_norm(t):
                dve.wait_ge(*upto("ln mean", t, 1))
                for i in range(NC):
                    V.tensor_tensor(DV[:, i, :], FL[:, i, :], PA[0:CC, 0:T], ALU.subtract)\
                        .then_inc(sem("dev"), 1)
                dve.wait_ge(*upto("ln ln", t, 1))
                V.tensor_scalar(VE[:, :], PB[0:CC, 0:T], LN_EPS, None, ALU.add).then_inc(sem("ln ve"), 1)
                dve.wait_ge(*upto("ln ve", t, 1))
                dve.wait_ge(*upto("ln y0", t, 1))
                link(V.tensor_tensor(YN[:, :], Y0[:, :], Y0[:, :], ALU.mult))
                link(V.scalar_tensor_tensor(out=YN[:, :], in0=YN[:, :], scalar=-0.5, in1=VE[:, :],
                                            op0=ALU.mult, op1=ALU.mult))
                link(V.scalar_tensor_tensor(out=YN[:, :], in0=YN[:, :], scalar=1.5, in1=Y0[:, :],
                                            op0=ALU.add, op1=ALU.mult))
                for i in range(NC):
                    V.tensor_tensor(SQ[:, i, :], DV[:, i, :], YN[:, :], ALU.mult).then_inc(sem("ln t"), 1)

            def hi_lo(src, hi, lo, src_ready, hi_signal, hi_ready, lo_signal):
                dve.wait_ge(*src_ready)
                V.tensor_copy(hi, src).then_inc(sem(hi_signal), 1)
                dve.wait_ge(*hi_ready)
                V.tensor_tensor(lo, src, hi.bitcast(F32), ALU.subtract).then_inc(sem(lo_signal), 1)

            def turned(part, psum, bias, ready):
                dve.wait_ge(*ready)
                for i in range(NC):
                    V.scalar_tensor_tensor(out=RF[part][:, i, :], in0=psum[0:CC, i * T:(i + 1) * T],
                                           scalar=vec(bias, i), in1=ROPE[:, part, :], op0=ALU.add, op1=ALU.mult)\
                        .then_inc(sem("dve chain"), 1)
                    n[0] += 1

            def rotated(dst, done):
                dve.wait_ge(sem("dve chain"), n[0])
                V.tensor_tensor(dst[:, :, :], RF[0][:, :, :], RF[1][:, :, :], ALU.add).then_inc(sem(done), 1)

            def queries_keys(l):
                def low_part(lo, part, hi, bias, ready, done):
                    for i in range(NC):
                        dve.wait_ge(*upto(ready, l, i + 1 if l == 2 else NC))
                        V.scalar_tensor_tensor(out=lo[:, i, :], in0=chunk_psum(part, l, i),
                                               scalar=vec(bias, i), in1=hi[:, i, :].bitcast(F32), op0=ALU.add,
                                               op1=ALU.subtract).then_inc(sem(done), 1)

                if l == 1:
                    loaded(dve, "rope")
                    turned(0, PA, "bq1", upto("q plain", 1, 1))
                    turned(1, PC[0], "bqp", upto("q psum", 1, 1))
                    rotated(QF, "qf")
                    dve.wait_ge(*upto("qf", 1, 1))
                    turned(0, PB, "bk1", upto("k plain", 1, 1))
                    dve.wait_ge(*upto("qh", 1, 1))
                    V.tensor_tensor(QL[:, :, :], QF[:, :, :], QH[:, :, :].bitcast(F32), ALU.subtract)\
                        .then_inc(sem("ql"), 1)
                    turned(1, PC[1], "bkp", upto("k psum", 1, 1))
                    rotated(KF, "kf")
                    hi_lo(KF[:, :, :], KH[:, :, :], KL[:, :, :], upto("kf", 1, 1), "kh", upto("kh", 1, 1), "kl")
                else:
                    if l == 2:
                        low_part(QL, "q", QH, "bq2", "qh", "ql")
                    else:
                        for g in range(NG):
                            dve.wait_ge(*upto("qf", l, g + 1))
                            V.tensor_copy(QB[:, 0, g, :], QD[:, g, :]).then_inc(sem("q b0"), 1)
                            V.tensor_copy(QHL[:, g, :], QD[:, g, :]).then_inc(sem("qh"), 1)
                        dve.wait_ge(*upto("q b0", l, NG))
                        V.tensor_tensor(QR[:, :, :], QD[:, :, :], QB[:, 0], ALU.subtract).then_inc(sem("q r"), 1)
                        dve.wait_ge(*upto("q r", l, 1))
                        V.tensor_copy(Q1[:, :, :], QR[0:64, :, :]).then_inc(sem("q1"), 1)
                        dve.wait_ge(*upto("q1", l, 1))
                        V.tensor_tensor(QB[0:64, 1], QR[0:64, :, :], Q1[:, :, :], ALU.subtract)\
                            .then_inc(sem("q b2"), 1)
                        dve.wait_ge(*upto("qh", l, NG))
                        V.tensor_tensor(QHL[64:128, :, :], QD[64:128, :, :], QHL[64:128, :, :].bitcast(F32),
                                        ALU.subtract).then_inc(sem("ql"), 1)
                    low_part(KL, "k", KH, f"bk{l}", "kh", "kl")
                if l in REL_LAYERS:
                    for w in range(2):
                        for b in range(2):
                            dve.wait_ge(*upto("rel h", l, 2 * w + b + 1))
                            V.tensor_tensor(rel_part(RL, w, b), rel_psum(w, b), rel_part(RH, w, b).bitcast(F32),
                                            ALU.subtract).then_inc(sem("rel l"), 1)
                dve.wait_ge(*upto("v psum", l, 1))
                if l == 0:
                    dve.wait_ge(sem("backgrounds"), 2)
                    loaded(dve, "vb")
                for c in range(2):
                    V.tensor_tensor(VX[:, c, :, 0:HD],
                                    slot("v", l, 0)[:, c * C:(c + 1) * C].rearrange("p (h d) -> p h d", h=NH),
                                    VB[:, l, :].rearrange("p (h d) -> p h d", h=NH), ALU.add)\
                        .then_inc(sem("v"), 1)

            def maximum(l, h):
                g = h // GH
                if g >= 2 and h % GH == 0:
                    dve.wait_ge(*upto("mt psum", l, g - 1))
                dve.wait_ge(*upto("max psum", l, h + 1))
                n_keys = WINDOW if l == 2 else T
                V.tensor_reduce(NM[g % 2][:, :, h % GH],
                                slot("m", l, h)[:, 0:2 * n_keys].rearrange("p (q k) -> p q k", q=2),
                                AX.X, ALU.max, negate=True).then_inc(sem("max"), 1)

            def unnormalised(l, g):
                dve.wait_ge(*upto("pv", l, GH * (g + 1)))
                if g >= 2:
                    dve.wait_ge(*upto("o", l, g - 1))
                V.tensor_copy(U[g % 2][:, :], PC[g % 2][:, 0:T]).then_inc(sem("u"), 1)

            def normalised(l, g):
                dve.wait_ge(*upto("rd", l, g + 1))
                link(V.scalar_tensor_tensor(out=LD[g % 2][:, :], in0=PC[g % 2][:, T:2 * T], scalar=-1.0,
                                            in1=RD[g % 2][:, :], op0=ALU.mult, op1=ALU.mult))
                link(V.scalar_tensor_tensor(out=LD[g % 2][:, :], in0=LD[g % 2][:, :], scalar=2.0,
                                            in1=RD[g % 2][:, :], op0=ALU.add, op1=ALU.mult))
                V.tensor_tensor(O[g][:, :], LD[g % 2][:, :], U[g % 2][:, :], ALU.mult).then_inc(sem("o"), 1)

            def registers():
                hi_lo(KRF[:, :, :], KRH[:, :, :], KRL[:, :, :], (sem("kr f"), NC), "kr parts", (sem("kr parts"), 1),
                      "kr parts")
                dve.wait_ge(sem("vr psum"), 1)
                V.tensor_tensor(VRB[:, :], slot("vr", 0, 0)[:, 0:C], VB[:, 2, :], ALU.add).then_inc(sem("vr"), 1)
                dve.wait_ge(sem("vr"), 1)
                dve.wait_ge(sem("backgrounds"), 7)
                loaded(dve, "pcol")
                for j in range(GH):
                    q = slice(32 * j, 32 * j + 32)
                    V.tensor_scalar(VR[q, j:NH:GH, 0:HD],
                                    VRB[q, :].rearrange("p (h d) -> p h d", h=NH)[:, j:NH:GH], PCOL[q, 2:3], None,
                                    ALU.mult).then_inc(sem("vr"), 1)
                    V.tensor_copy(VR[q, j:NH:GH, HD:32], PCOL[q, 2:3, None].to_broadcast([32, NG, HD]))\
                        .then_inc(sem("vr"), 1)

            selectors()
            loaded(dve, "x")
            for l in range(LAYERS):
                group_norm(l, FL if l == 1 else XN)
                if l == 0:
                    loaded(dve, "vecs")
                    rel_parts()
                if l == 1:
                    layer_norm(1)
                queries_keys(l)
                if l == 0:
                    registers()
                    bias_cols()
                    reg_selector()
                for h in range(NH):
                    maximum(l, h)
                for g in range(NG):
                    unnormalised(l, g)
                    normalised(l, g)
                dve.wait_ge(*upto("y psum", l, 1))
                if l != 1:
                    for i in range(NC):
                        ins = V.scalar_tensor_tensor(out=X[:, i, :], in0=PB[0:CC, i * T:(i + 1) * T],
                                                     scalar=vec(f"bo{l}", i), in1=X[:, i, :],
                                                     op0=ALU.add, op1=ALU.add)
                        ins.then_inc(sem("x"), 1)
                else:
                    for i in range(NC):
                        V.scalar_tensor_tensor(out=FL[:, i, :], in0=PB[0:CC, i * T:(i + 1) * T],
                                               scalar=vec("bo1", i), in1=FL[:, i, :],
                                               op0=ALU.add, op1=ALU.add).then_inc(sem("x"), 1)
                    dve.wait_ge(*upto("x", 1, NC))
                    layer_norm(3)
                    dve.wait_ge(sem("ff psum"), 1)
                    for i in range(NC):
                        V.scalar_tensor_tensor(out=FL[:, i, :], in0=PA[0:CC, i * T:(i + 1) * T],
                                               scalar=vec("b2", i), in1=FL[:, i, :],
                                               op0=ALU.add, op1=ALU.add).then_inc(sem("x"), 1)
                    dve.wait_ge(*upto("x", 1, 2 * NC))
                    for i in range(NC):
                        V.tensor_tensor(X[:, i, :], X[:, i, :], FL[:, i, :], ALU.add).then_inc(sem("x"), 1)

        @block.tensor
        def _(pe):
            M = nc.tensor.matmul

            def keep_warm(bank, n):
                for _ in range(n):
                    M(bank, WARM[:, 0:P], WARM[:, :], start=True, stop=True)

            def take(*use):
                if number[use] >= 2:
                    former = uses[RING_OF[use[0]]][number[use] - 2]
                    for name, count in readers(*former):
                        pe.wait_ge(*upto(name, former[1], count))
                return slot(*use)

            def chunk_ready(ready, n_ready, k):
                pe.wait_ge(ready, n_ready - NC + k + 1)

            def project(chunk, w, c0, src, ready, n_ready, done=None):
                for m in range(NC):
                    for k in range(NC):
                        chunk_ready(ready, n_ready, k)
                        ins = M(chunk(m), w[:, k, c0 + m * CC:c0 + (m + 1) * CC], src[:, k, :],
                                start=(k == 0), stop=(k == NC - 1))
                    if m < NC - 1 and done:
                        ins.then_inc(sem(done), 1)
                return ins

            def relative(l):
                pe.wait_ge(sem("rel b1"), 1)
                pe.wait_ge(sem("rel b2"), 1)
                pe.wait_ge(*upto("q b0 copy", l, 1))
                pe.wait_ge(*upto("q b1", l, 1))
                pe.wait_ge(*upto("q b2", l, 1))
                for w in range(2):
                    if w == 1:
                        pe.wait_ge(*upto("q cols", l, 2))
                    table = 2 * REL_LAYERS.index(l) + w
                    for i in range(SIDE):
                        terms = PC[i // 8][64 * w:64 * w + 64, i % 8 * NG * SIDE:(i % 8 + 1) * NG * SIDE]
                        for t, (qp, tp) in enumerate(TERMS):
                            lhsT = RELB[:, tp, table, (SIDE - 1 - i) * GH:(NREL - i) * GH]
                            q = QB[:, qp, :, i * SIDE:(i + 1) * SIDE] if w == 0 else QC[:, qp * NG:(qp + 1) * NG, i, :]
                            ins = M(terms.rearrange("p (g c) -> p g c", g=NG), lhsT, q, start=(t == 0),
                                    stop=(t == len(TERMS) - 1))
                        if i % 8 == 7:
                            ins.then_inc(sem("rel psum"), 1)

            def for_maxima(l, h):
                s = take("m", l, h)
                for q in range(2):
                    if l == 2:
                        keys = slice(0, WINDOW) if q == 0 else slice(REG1 + NREG - WINDOW, REG1 + NREG)
                    else:
                        keys = slice(KEY0, REG1)
                    n_keys = keys.stop - keys.start
                    ins = M(s[:, q * n_keys:(q + 1) * n_keys], QS[l % 2][:, h, q * P:(q + 1) * P], KS[:, h, keys],
                            start=True, stop=True)
                ins.then_inc(sem("max psum"), 1)

            def turn_early(l):
                pe.wait_ge(*upto("max", l, EARLY))
                pe.wait_ge(sem("idr"), 1)
                pe.wait_ge(sem("sels"), 1)
                for q in range(2):
                    ins = M(PA[0:EARLY, q * P:(q + 1) * P], NM[0][:, q, 0:EARLY], IDR[:, :], start=True, stop=True)
                ins.then_inc(sem("early psum"), 1)

            def turn_maxima(l, g):
                pe.wait_ge(*upto("max", l, GH * (g + 1)))
                pe.wait_ge(*(upto("mt", l, g) if g else upto("early", l, 1)))
                for q in range(2):
                    ins = M(PA[:, q * P:(q + 1) * P], NM[g % 2][:, q, :], IDR[:, :], start=True, stop=True)
                ins.then_inc(sem("mt psum"), 1)

            def reg_scores(l, g):
                s = take("r", l, g)
                pe.wait_ge(sem("sels"), 2)
                pe.wait_ge(*upto("mt", l, g + 1))
                for j in range(GH):
                    dst = s[32 * j:32 * j + 32, 0:T]
                    M(dst, KS[:, GH * g + j, REG1:KW].bitcast(F32), QS[l % 2][:, GH * g + j, :].bitcast(F32),
                      start=True, stop=False)
                    ins = M(dst, SELR[:, j, :], MT[g % 2][:, :].bitcast(F32), start=False, stop=True)
                ins.then_inc(sem("reg psum"), 1)

            def scores(l, h):
                s = take("e", l, h)
                if h < EARLY:
                    pe.wait_ge(*upto("early", l, 1))
                    sel, mt = SELM[0:EARLY, h, :], MT[1][0:EARLY, :]
                else:
                    pe.wait_ge(*upto("mt", l, h // GH + 1))
                    sel, mt = SELM[:, h % GH, :], MT[h // GH % 2][:, :]
                for k in range(2):
                    dst = s[:, k * T:(k + 1) * T]
                    M(dst, KS[:, h, KEY0 + k * P:KEY0 + (k + 1) * P], QS[l % 2][:, h, :], start=True, stop=False)
                    ins = M(dst, sel, mt, start=False, stop=True)
                ins.then_inc(sem("scores"), 1)

            def values(l, h):
                g, j = h // GH, h % GH
                pe.wait_ge(*upto("probs", l, h + 1))
                if h == 0:
                    pe.wait_ge(*upto("v", l, 2))
                    if l == 2:
                        pe.wait_ge(sem("vr"), 1 + 2 * GH)
                if j == 0 and g >= 2:
                    pe.wait_ge(*upto("o", l, g - 1))
                if j == 0 and l == 2:
                    pe.wait_ge(*upto("reg probs", l, g + 1))
                dst = PC[g % 2][32 * j:32 * j + 32, 0:T]
                for k in range(2):
                    ins = M(dst, VX[:, k, h, :], PR[:, h % NPR, k * T:(k + 1) * T], start=(k == 0),
                            stop=(k == 1 and l != 2))
                if l == 2:
                    ins = M(dst, VR[:, h, :], PG[g % 2][:, :], start=False, stop=True)
                ins.then_inc(sem("pv"), 1)

            def row_sums(l, g):
                if l == 0 and g == 0:
                    loaded(pe, "bsel")
                pe.wait_ge(*upto("u", l, g + 1))
                M(PC[g % 2][:, T:2 * T], BSEL[:, :], U[g % 2][:, :], start=True, stop=True)\
                    .then_inc(sem("d psum"), 1)

            def out_project(l, g):
                if g == 0:
                    loaded(pe, f"wo{l}")
                pe.wait_ge(*upto("o", l, g + 1))
                for m in range(NC):
                    ins = M(PB[0:CC, m * T:(m + 1) * T], WO[l][:, g, m * CC:(m + 1) * CC], O[g][:, :],
                            start=(g == 0 and m == 0), stop=(g == NG - 1), skip_group_check=True)
                if g == NG - 1:
                    ins.then_inc(sem("y psum"), 1)

            def registers():
                s = take("kr", 0, 0)
                loaded(pe, "w2", "regt")
                pe.wait_ge(sem("k scaled"), 2 + SCALED.index("w2"))
                for m in range(NC):
                    for k in range(NC):
                        ins = M(s[0:CC, m * NREG:(m + 1) * NREG], WQKV[2][:, k, C + m * CC:C + (m + 1) * CC],
                                REGT[:, k, 0:NREG], start=(k == 0), stop=(k == NC - 1))
                ins.then_inc(sem("kr psum"), 1)
                s = take("vr", 0, 0)
                for k in range(NC):
                    ins = M(s[:, 0:C], REGT[:, k, :], WQKV[2][:, k, 2 * C:3 * C], start=(k == 0),
                            stop=(k == NC - 1))
                ins.then_inc(sem("vr psum"), 1)

            def layer_norm(t, free, ready, n_ready):
                pe.wait_ge(ready, n_ready)
                for k in range(NC):
                    ins = M(PA[0:CC, 0:T], ONESC[:, :], FL[:, k, :], start=(k == 0), stop=(k == NC - 1))
                ins.then_inc(sem("ln mean"), 1)
                keep_warm(free, 4)
                for k in range(NC):
                    pe.wait_ge(*upto("sq", t, k + 1))
                    ins = M(PB[0:CC, 0:T], ONESC[:, :], SQ[:, k, :], start=(k == 0), stop=(k == NC - 1))
                ins.then_inc(sem("ln var psum"), 1)
                keep_warm(free, 16)

            def take_free(l):
                pe.wait_ge(*upto("probs", l, NH - 1))
                return slot("e", l, NH - 2)[:, :]

            pe.wait_ge(sem("warm"), 1)
            for l in range(LAYERS):
                free = take("v", l, 0)[:, :]
                keep_warm(free, 9 if l == 0 else 10)
                if l == 0:
                    loaded(pe, "gavg")
                pe.wait_ge(*upto("stats", l, NC))
                M(PA[0:CC, 0:2 * NC], GAVG[:, :], MS[:, :, :], start=True, stop=True)\
                    .then_inc(sem("gstats"), 1)
                keep_warm(free, 7)
                ready = upto("xn", l, NC)
                if l == 1:
                    pe.wait_ge(sem("backgrounds"), 7)
                    layer_norm(1, free, *ready)
                    ready = upto("ni", 1, NC)
                loaded(pe, f"w{l}")
                if l in REL_LAYERS:
                    for g in range(NG):
                        dst = q_psum(l, g) if g < 2 else take("q", l, 0)[:, 0:T]
                        for k in range(NC):
                            chunk_ready(*ready, k)
                            ins = M(dst, WQKV[l][:, k, g * P:(g + 1) * P], XN[:, k, :], start=(k == 0),
                                    stop=(k == NC - 1))
                        ins.then_inc(sem("q psum"), 1)
                else:
                    last = project(lambda m: chunk_psum("q", l, m), WQKV[l], 0, XN, *ready, "q psum" if l == 2 else None)
                    if l == 1:
                        last.then_inc(sem("q plain"), 1)
                        loaded(pe, "wp")
                        last = project(lambda m: PC[0][0:CC, m * T:(m + 1) * T], WP, 0, XN, *ready)
                    last.then_inc(sem("q psum"), 1)
                pe.wait_ge(sem("k scaled"), 2 + SCALED.index("wp" if l == 1 else f"w{l}"))
                last = project(lambda m: chunk_psum("k", l, m), WQKV[l], key_column(l), XN, *ready,
                               "k psum" if l == 2 else None)
                if l == 1:
                    last.then_inc(sem("k plain"), 1)
                    last = project(lambda m: PC[1][0:CC, m * T:(m + 1) * T], WP, C, XN, *ready)
                last.then_inc(sem("k psum"), 1)
                s = take("v", l, 0)
                for c in range(2):
                    for k in range(NC):
                        ins = M(s[:, c * C:(c + 1) * C], XN[:, k, c * P:(c + 1) * P],
                                WQKV[l][:, k, key_column(l) + C:key_column(l) + 2 * C], start=(k == 0), stop=(k == NC - 1))
                ins.then_inc(sem("v psum"), 1)
                if l in REL_LAYERS:
                    keep_warm(take("m" if l else "kr", l, 0)[:, :], 2)
                    relative(l)

                if l == 0:
                    registers()
                    pe.wait_ge(sem("hot rows"), 16)
                    pe.wait_ge(sem("zero rows"), 48)
                    pe.wait_ge(sem("backgrounds"), 4)
                if l == 1:
                    pe.wait_ge(sem("ab rows"), NH)
                if l == 2:
                    pe.wait_ge(sem("mask rows"), 16)
                    pe.wait_ge(sem("kr stack"), 6 * 16)
                keep_warm(take("m", l, 0)[:, :], DMA_WARM[l])
                pe.wait_ge(*upto("q stack", l, signals["q stack"][l]))
                pe.wait_ge(*upto("k stack", l, 48))
                if l in REL_LAYERS:
                    pe.wait_ge(*upto("rel stack", l, 64))

                for h in range(EARLY + 1):
                    for_maxima(l, h)
                    keep_warm(PB[:, :], 2 if h == 1 else 0)
                turn_early(l)
                for_maxima(l, EARLY + 1)
                ahead = EARLY + 2
                for h in range(NH):
                    g, j = h // GH, h % GH
                    if l == 2 and h in (EARLY, GH, 2 * GH):
                        reg_scores(l, g)
                    if h == GH - 1:
                        turn_maxima(l, 1)
                    scores(l, h)
                    wanted = min(h + AHEAD + 1, NH) if h >= EARLY else ahead + 1
                    if ahead < wanted:
                        for_maxima(l, ahead)
                        ahead += 1
                    if h == EARLY - 1:
                        turn_maxima(l, 0)
                        for_maxima(l, ahead)
                        ahead += 1
                    if h == GH + 2:
                        turn_maxima(l, 2)
                    if h == GH + 2:
                        row_sums(l, 0)
                    if h >= 2:
                        values(l, h - 2)
                    for m in range(ahead, wanted):
                        for_maxima(l, m)
                    ahead = max(ahead, wanted)
                    if h == 2 * GH + 2:
                        row_sums(l, 1)
                values(l, NH - 2)
                values(l, NH - 1)
                out_project(l, 0)
                row_sums(l, 2)
                out_project(l, 1)
                keep_warm(take_free(l), 7)
                out_project(l, 2)
                if l == 1:
                    free = take("f", 1, 0)[:, :]
                    keep_warm(free, 4)
                    layer_norm(3, free, *upto("x", 1, NC))
                    loaded(pe, "ff1", "ff2")
                    pe.wait_ge(*upto("ni", 3, NC))
                    for m in range(FM // 2):
                        s = take("f", 1, m)
                        for i in range(2):
                            for k in range(NC):
                                c = 2 * m + i
                                ins = M(s[:, i * T:(i + 1) * T], W1[:, k, c * P:(c + 1) * P], XN[:, k, :], start=(k == 0),
                                        stop=(k == NC - 1))
                        ins.then_inc(sem("hid psum"), 1)
                    for c in range(FM):
                        pe.wait_ge(sem("hid"), c + 1)
                        for m in range(NC):
                            ins = M(PA[0:CC, m * T:(m + 1) * T], W2[:, c, m * CC:(m + 1) * CC], hidden(c),
                                    start=(c == 0 and m == 0), stop=(c == FM - 1), skip_group_check=True)
                    ins.then_inc(sem("ff psum"), 1)


def layouts(inp):
    f32 = np.float32
    heads = np.arange(NH)

    order = np.arange(C).reshape(HPC, NC, HD).transpose(1, 2, 0).reshape(C)

    order2 = np.arange(C).reshape(GH, NG, HD).transpose(1, 2, 0).reshape(NG, 64)

    def qk_order(l, w):
        q = w[..., np.tile(order2, (1, 2)).reshape(Q2)] if l in REL_LAYERS else w[..., order]
        return np.concatenate([q, w[..., C + order], w[..., 2 * C:]], -1)

    def chunks(w):
        return np.ascontiguousarray(w.reshape(NC, CC, -1).transpose(1, 0, 2))

    def column(v):
        return v.reshape(NC, CC).T

    def by_quadrant(w):
        padded = np.zeros((NG, GH, 32, C), f32)
        padded[:, :, :HD] = w.reshape(NG, GH, HD, C)
        return np.ascontiguousarray(padded.transpose(1, 2, 0, 3).reshape(P, NG, C))

    def swapped(w):
        return w.reshape(*w.shape[:-1], NH, 2, HD // 2)[..., ::-1, :].reshape(w.shape)

    def toeplitz(rel):
        t = np.zeros((2, HD, GH, 32, GH), f32)
        for j in range(GH):
            t[:, :, j, :NREL, j] = rel[:NREL][::-1].T
        return t.reshape(P, GH * 32)

    L = {k: np.asarray(v) for k, v in inp.items()}
    wqkv = [L["L0_conv_qkv_w"], np.concatenate([L["L1_conv_wq"], L["L1_conv_wk"], L["L1_conv_wv"]], 1),
            L["L2_conv_qkv_w"].T, L["L3_conv_qkv_w"].T]
    bqkv = [L["L0_conv_qkv_b"], np.concatenate([L["L1_conv_bq"], L["L1_conv_bk"], L["L1_conv_bv"]]),
            L["L2_conv_qkv_b"], L["L3_conv_qkv_b"]]
    wqkv = [qk_order(l, w) for l, w in enumerate(wqkv)]
    bqkv = [qk_order(l, b) for l, b in enumerate(bqkv)]
    wo = [L["L0_conv_proj_w"], L["L1_conv_wo"], L["L2_conv_out_w"].T, L["L3_conv_proj_w"].T]
    bo = [L["L0_conv_proj_b"], L["L1_conv_bo"], L["L2_conv_out_b"], L["L3_conv_proj_b"]]

    vecs = np.zeros((CC, 2 * len(VEC)), f32)
    named = {f"bk{l}": bqkv[l][-2 * C:-C] for l in range(LAYERS)}
    named |= {f"bq{l}": bqkv[l][:C] for l in (1, 2)}
    named |= {f"bo{l}": bo[l] for l in range(LAYERS)}
    named |= {"bqp": swapped(L["L1_conv_bq"])[order], "bkp": swapped(L["L1_conv_bk"])[order], "ln1g": L["L1_conv_ln1_g"],
              "ln1b": L["L1_conv_ln1_b"], "ln3g": L["L1_conv_ln3_g"], "ln3b": L["L1_conv_ln3_b"],
              "b2": L["L1_conv_b2"]}
    for name, v in named.items():
        vecs[:, VEC[name]:VEC[name] + NC] = column(v)

    place = np.arange(T)
    row, col, k = place // SIDE, place % SIDE, np.arange(SIDE)[:, None]
    hot = np.zeros((P, T), f32)
    hot[64:80] = hot[96:112] = row == k
    hot[80:96] = hot[112:128] = col == k
    first = np.clip(np.arange(SIDE) - 3, 0, SIDE - 7)
    mask = np.zeros((P, T), f32)
    mask[64:80] = np.where((k >= first[row]) & (k < first[row] + 7), 0, MASKED)
    mask[80:96] = np.where((k >= first[col]) & (k < first[col] + 7), 0, MASKED)
    angles = HD // 4
    timescale = np.concatenate([f32(10000.0) ** (f32(2) * np.arange(angles, dtype=f32) / f32(HD)),
                                np.full(HD // 2 - angles, np.inf, f32)]).astype(f32)
    angle = (place.astype(f32)[:, None] / timescale).astype(f32)
    sin, cos = np.sin(angle).T, np.cos(angle).T
    rope = np.stack([np.repeat(np.concatenate([cos, cos]), HPC, 0), np.repeat(np.concatenate([-sin, sin]), HPC, 0)], 1)
    group = np.arange(CC) // GN_GROUP
    pcol = np.zeros((P, 3), f32)
    pcol[64:80, 0] = 1
    pcol[96:112, 1] = 1
    pcol[:, 2] = np.arange(P) % 32 < NREG
    bsel = np.zeros((P, P), f32)
    for j in range(GH):
        bsel[32 * j + HD, 32 * j:32 * j + 32] = 1
    abt = np.zeros((P, 2, NH), f32)
    abt[64:128] = L["L1_conv_attn_biases"].T
    regt = np.zeros((CC, NC, GH, 32), f32)
    regt[:, :, :, :NREG] = chunks(L["L2_conv_registers"].T)[:, :, None, :]

    arrays = {"xT": chunks(L["x"].reshape(T, C).T), "vecs": vecs, "gavg": (group[:, None] == group) / f32(GN_GROUP),
              "pcol": pcol, "relt": np.stack([toeplitz(L[f"L{l}_conv_rel_pos_{v}"]) for l in REL_LAYERS for v in "hw"], 1),
              "hot": hot, "zeros": np.zeros((HD, NH, T), f32), "mask": mask, "abt": abt, "bsel": bsel, "rope": rope, "regt": regt.reshape(CC, NC, P),
              "qbias": np.stack([bqkv[l][:Q2].reshape(NG, P).T for l in REL_LAYERS], 1),
              "vb": np.broadcast_to(np.stack([b[-C:] for b in bqkv]), (P, LAYERS, C)),
              "wp": chunks(np.concatenate([swapped(L["L1_conv_wq"])[:, order], swapped(L["L1_conv_wk"])[:, order]], 1)),
              "ff1": chunks(L["L1_conv_w1"]), "ff2": L["L1_conv_w2"].reshape(FM, P, C).transpose(1, 0, 2),
              "b1": L["L1_conv_b1"].reshape(FM, P).T}
    for l in range(LAYERS):
        arrays[f"w{l}"] = chunks(wqkv[l])
        arrays[f"wo{l}"] = by_quadrant(wo[l])
    return {name: np.ascontiguousarray(v, dtype=f32) for name, v in arrays.items()}


def kernel(**inputs):
    import concourse.bacc as bacc
    from concourse.bass_utils import run_bass_kernel_spmd

    nc = bacc.Bacc("TRN2", target_bir_lowering=False, num_devices=1)
    arrays = layouts(inputs)
    args = {name: nc.dram_tensor(f"in_{name}", v.shape, F32, kind="ExternalInput").ap() for name, v in arrays.items()}
    out = nc.dram_tensor("out_xT", (CC, NC, T), F32, kind="ExternalOutput").ap()
    build(nc, args, out)
    r = run_bass_kernel_spmd(nc, [{f"in_{name}": v for name, v in arrays.items()}], core_ids=[0])
    got = r.results[0]["out_xT"]
    return got.transpose(2, 1, 0).reshape(1, SIDE, SIDE, C)
```
